# Optimizing a Trainium2 kernel written in Bass

```python
import numpy as np
import jax
import jax.numpy as jnp

def _softmax(x, axis=-1):
    return jax.nn.softmax(x, axis=axis)

def _gelu(x):
    return jax.nn.gelu(x, approximate=True)

def _silu(x):
    return jax.nn.silu(x)

def _sigmoid(x):
    return jax.nn.sigmoid(x)

def _layernorm(x, axis=-1, eps=1e-05):
    m = jnp.mean(x, axis=axis, keepdims=True)
    v = jnp.var(x, axis=axis, keepdims=True)
    return (x - m) / jnp.sqrt(v + eps)

def _scatter_add(tgt, idx, src, axis=0):
    return tgt.at[idx].add(src)

def _segment_sum(src, seg, n):
    return jax.ops.segment_sum(src, seg, n)
kernel_name = 'mk_cond_resid_d4_seqx_r4_222000'

def setup_inputs(seed: int=0):
    np.random.seed(seed)
    _w = jnp.asarray

    def _rec_inputs():
        import jax
        import jax.numpy as jnp
        _rk = jax.random.key(seed)
        x = -7.109e-05 + 0.9999 * jax.random.normal(jax.random.fold_in(_rk, 1), (64, 64, 512), jnp.float32)
        _lenS = 64 - jax.random.randint(jax.random.fold_in(_rk, 7), (64,), 0, max(1, 64 // 4) + 1, jnp.int32)
        _lenS2 = 64 - jax.random.randint(jax.random.fold_in(_rk, 8), (64,), 0, max(1, 64 // 4) + 1, jnp.int32)
        itok_B_0_6 = jax.random.randint(jax.random.fold_in(_rk, 11), (64,), 0, 7, jnp.int32)
        itok_B_1_198 = jax.random.randint(jax.random.fold_in(_rk, 12), (64,), 1, 199, jnp.int32)
        cond_1 = jax.random.uniform(jax.random.fold_in(_rk, 13), (64, 1), jnp.float32, 0.0, 1.37214)
        itok_B_0_7 = jax.random.randint(jax.random.fold_in(_rk, 14), (64,), 0, 8, jnp.int32)
        return (x, itok_B_0_6, itok_B_1_198, cond_1, itok_B_0_7)
    x, itok_B_0_6, itok_B_1_198, cond_1, itok_B_0_7 = _rec_inputs()

    def _L0_cond_setup():
        import jax, jax.numpy as jnp
        import numpy as np
        B, T, D_IN, D_OUT = (16, 512, 512, 512)
        N_ADAPTERS, RANK = (8, 16)
        key = jax.random.key(seed)
        k_x, k_w, k_a, k_b, k_s, k_idx = jax.random.split(key, 6)
        x = jax.random.normal(k_x, (B, T, D_IN), dtype=jnp.float32)
        W = jax.random.normal(k_w, (D_OUT, D_IN), dtype=jnp.float32) * (1.0 / np.sqrt(D_IN))
        A = jax.random.normal(k_a, (N_ADAPTERS, RANK, D_IN), dtype=jnp.float32) * 0.02
        Bm = jax.random.normal(k_b, (N_ADAPTERS, D_OUT, RANK), dtype=jnp.float32) * 0.02
        scalings = jnp.ones((N_ADAPTERS,), dtype=jnp.float32)
        adapter_idx = jax.random.randint(k_idx, (B,), 0, N_ADAPTERS, dtype=jnp.int32)
        return {'x': x, 'W': W, 'A': A, 'Bm': Bm, 'scalings': scalings, 'adapter_idx': adapter_idx}
    _L0_cond_all = _L0_cond_setup()
    _L0_cond_in = {k: v for k, v in _L0_cond_all.items() if k in ('W', 'A', 'Bm', 'scalings')}
    del _L0_cond_all

    def _L1_cond_setup():
        import jax, jax.numpy as jnp
        import numpy as np
        B, C, T = (128, 64, 512)
        S, D = (200, 64)
        key = jax.random.key(seed)
        k1, k2, k3 = jax.random.split(key, 3)
        x = jax.random.normal(k1, (B, C, T), dtype=jnp.float32)
        conditions = jax.random.randint(k2, (B,), 0, S, dtype=jnp.int64)
        weights = jax.random.normal(k3, (S, C, D), dtype=jnp.float32) / jnp.sqrt(jnp.float32(C))
        return {'x': x, 'conditions': conditions, 'weights': weights}
    _L1_cond_all = _L1_cond_setup()
    _L1_cond_in = {k: v for k, v in _L1_cond_all.items() if k in ('weights',)}
    del _L1_cond_all

    def _L2_cond_setup():
        import jax, jax.numpy as jnp
        import numpy as np
        B, S, D_MODEL, NHEAD = (4, 512, 512, 16)
        HEAD_DIM = D_MODEL // NHEAD
        key = jax.random.key(seed)
        ks = jax.random.split(key, 6)
        scale = 1.0 / np.sqrt(D_MODEL)
        return {'hidden_states': jax.random.normal(ks[0], (B, S, D_MODEL), dtype=jnp.float32), 'attention_precision': jax.random.uniform(ks[1], (B, 1, 1), dtype=jnp.float32, minval=0.5, maxval=2.0), 'Wq': jax.random.normal(ks[2], (D_MODEL, D_MODEL), dtype=jnp.float32) * scale, 'Wk': jax.random.normal(ks[3], (D_MODEL, D_MODEL), dtype=jnp.float32) * scale, 'Wv': jax.random.normal(ks[4], (D_MODEL, D_MODEL), dtype=jnp.float32) * scale, 'Wo': jax.random.normal(ks[5], (D_MODEL, D_MODEL), dtype=jnp.float32) * scale}
    _L2_cond_all = _L2_cond_setup()
    _L2_cond_in = {k: v for k, v in _L2_cond_all.items() if k in ('Wq', 'Wk', 'Wv', 'Wo')}
    del _L2_cond_all

    def _L3_cond_setup():
        import jax, jax.numpy as jnp
        import numpy as np
        B, C, D, T, N_SUBJECTS = (128, 64, 64, 512, 8)
        key = jax.random.key(seed)
        kx, ks, kw = jax.random.split(key, 3)
        x = jax.random.normal(kx, (B, C, T), dtype=jnp.float32)
        subjects = jax.random.randint(ks, (B,), 0, N_SUBJECTS, dtype=jnp.int64)
        weights = jax.random.normal(kw, (N_SUBJECTS, C, D), dtype=jnp.float32) * (1.0 / C ** 0.5)
        return {'x': x, 'subjects': subjects, 'weights': weights}
    _L3_cond_all = _L3_cond_setup()
    _L3_cond_in = {k: v for k, v in _L3_cond_all.items() if k in ('weights',)}
    del _L3_cond_all
    return {'x': x, 'itok_B_0_6': itok_B_0_6, 'itok_B_1_198': itok_B_1_198, 'cond_1': cond_1, 'itok_B_0_7': itok_B_0_7, 'L0_cond_W': _L0_cond_in['W'], 'L0_cond_A': _L0_cond_in['A'], 'L0_cond_Bm': _L0_cond_in['Bm'], 'L0_cond_scalings': _L0_cond_in['scalings'], 'L1_cond_weights': _L1_cond_in['weights'], 'L2_cond_Wq': _L2_cond_in['Wq'], 'L2_cond_Wk': _L2_cond_in['Wk'], 'L2_cond_Wv': _L2_cond_in['Wv'], 'L2_cond_Wo': _L2_cond_in['Wo'], 'L3_cond_weights': _L3_cond_in['weights']}

def reference(x, itok_B_0_6, itok_B_1_198, cond_1, itok_B_0_7, L0_cond_W, L0_cond_A, L0_cond_Bm, L0_cond_scalings, L1_cond_weights, L2_cond_Wq, L2_cond_Wk, L2_cond_Wv, L2_cond_Wo, L3_cond_weights):
    import jax
    import jax.numpy as jnp

    def _L0_cond_ref(x, W, A, Bm, scalings, adapter_idx):
        import jax, jax.numpy as jnp
        import numpy as np
        B, T, D_IN, D_OUT = (16, 512, 512, 512)
        N_ADAPTERS, RANK = (8, 16)
        H = jnp.einsum('btd,od->bto', x, W)
        A_b = A[adapter_idx]
        B_b = Bm[adapter_idx]
        s_b = scalings[adapter_idx]
        xa = jnp.einsum('btd,brd->btr', x, A_b)
        delta = jnp.einsum('btr,bor->bto', xa, B_b)
        delta = jax.lax.stop_gradient(delta * s_b[:, None, None])
        return H + delta

    def _L1_cond_ref(x, conditions, weights):
        import jax, jax.numpy as jnp
        import numpy as np
        B, C, T = (128, 64, 512)
        S, D = (200, 64)
        w = weights[conditions]
        return jnp.einsum('bct,bcd->bdt', x, w)

    def _L2_cond_ref(hidden_states, attention_precision, Wq, Wk, Wv, Wo):
        import jax, jax.numpy as jnp
        import numpy as np
        B, S, D_MODEL, NHEAD = (4, 512, 512, 16)
        HEAD_DIM = D_MODEL // NHEAD
        b, s, _ = hidden_states.shape

        def proj(x, W):
            y = jnp.einsum('bsd,ed->bse', x, W)
            return y.reshape(b, s, NHEAD, HEAD_DIM).transpose(0, 2, 1, 3)
        q = proj(hidden_states, Wq)
        k = proj(hidden_states, Wk)
        v = proj(hidden_states, Wv)
        beta = jnp.minimum(attention_precision, 4.0)[:, None]
        q = q * beta
        scores = jnp.einsum('bhqd,bhkd->bhqk', q, k) / np.sqrt(HEAD_DIM)
        causal = jnp.tril(jnp.ones((s, s), dtype=bool))
        scores = jnp.where(causal, scores, jnp.finfo(scores.dtype).min)
        attn = jax.nn.softmax(scores, axis=-1)
        out = jnp.einsum('bhqk,bhkd->bhqd', attn, v)
        out = out.transpose(0, 2, 1, 3).reshape(b, s, D_MODEL)
        return jnp.einsum('bsd,ed->bse', out, Wo)

    def _L3_cond_ref(x, subjects, weights):
        import jax, jax.numpy as jnp
        import numpy as np
        B, C, D, T, N_SUBJECTS = (128, 64, 64, 512, 8)
        w = weights[subjects]
        out = jnp.einsum('bct,bcd->bdt', x, w)
        return out
    x = x + _L0_cond_ref(x, L0_cond_W, L0_cond_A, L0_cond_Bm, L0_cond_scalings, itok_B_0_6)
    x = x + _L1_cond_ref(x, itok_B_1_198, L1_cond_weights)
    x = x + _L2_cond_ref(x, cond_1[:, None, :], L2_cond_Wq, L2_cond_Wk, L2_cond_Wv, L2_cond_Wo)
    x = x + _L3_cond_ref(x, itok_B_0_7, L3_cond_weights)
    return x

_drawn_inputs = setup_inputs


def setup_inputs(seed=0):
    import zlib

    import numpy as np

    out = dict(_drawn_inputs(seed))
    spreads = {'L0_cond_scalings': (1.0, 0.6)}
    factors = {}
    for name, (base, spread) in spreads.items():
        noise = np.random.default_rng([zlib.crc32(name.encode()), seed]).standard_normal(out[name].shape)
        drawn = base * np.exp(spread * noise) if base else spread * noise
        out[name] = jnp.asarray(drawn.astype(out[name].dtype))
    for name, factor in factors.items():
        out[name] = (out[name] * factor).astype(out[name].dtype)
    return out
```

```python
import math
from contextlib import ExitStack

import concourse.bass as bass
from concourse import mybir

F32 = mybir.dt.float32
F32R = mybir.dt.float32r
I32 = mybir.dt.int32
ALU = mybir.AluOpType
ACT = mybir.ActivationFunctionType
AX = mybir.AxisListType

P = 128
SEQS, S, D = 64, 64, 512
NC = D // P
TILES = 2
PT = TILES * P
PAIRS = SEQS * S // PT
PSEQ = PT // S
SEQT = P // S
HEADS, HD = 16, 32
HP = HEADS // 2
ADAPTERS, RANK = 8, 16
MASKED = -1.0e30
BETA_MAX = 4.0
BANK = 512
NW = 5
W0, WQ, WK, WV, WO = range(NW)
LOADED = (W0, WK, WQ, WV, WO)
STAGES = 3


def cond_resid_kernel(nc, x, idx0, idx1, cond, idx3, W, A, Bm, scal, w1, Wq, Wk, Wv, Wo, w3, out):
    weights = {W0: W, WQ: Wq, WK: Wk, WV: Wv, WO: Wo}
    x_v = x.rearrange("(i t b) s d -> i (b s) t d", t=TILES, b=SEQT)
    out_v = out.rearrange("(i t b) s d -> i (b s) t d", t=TILES, b=SEQT)

    with ExitStack() as ctx:
        def sb(name, shape, dt=F32):
            return ctx.enter_context(nc.sbuf_tensor(name, shape, dt))

        def sem(name):
            return ctx.enter_context(nc.semaphore(name))

        ctx.enter_context(nc.allow_non_contiguous_dma(reason="a few small tables are loaded once"))

        ident = sb("ident", [P, P])
        mask = sb("mask", [P, S])
        block_mask = sb("block_mask", [P, P])
        row_number = sb("row_number", [P, 1], I32)
        adapter_of_row = sb("adapter_of_row", [P, 1], I32)
        adapter_of_row_f = sb("adapter_of_row_f", [P, 1])
        scal_of_row = sb("scal_of_row", [P, 1])
        idx0_all = sb("idx0_all", [P, SEQS], I32)
        idx0_f = sb("idx0_f", [P, SEQS])
        adapter_scale = sb("adapter_scale", [P, SEQS])
        idx1_row = sb("idx1_row", [1, SEQS], I32)
        idx3_row = sb("idx3_row", [1, SEQS], I32)
        cond_all = sb("cond_all", [P, SEQS])
        beta = sb("beta", [P, PAIRS * TILES])
        w_hi = sb("w_hi", [P, NW, NC, D], F32R)
        w_lo = sb("w_lo", [P, NW, NC, D], F32R)
        a_hi = sb("a_hi", [P, NC, P], F32R)
        a_lo = sb("a_lo", [P, NC, P], F32R)
        b_hi = sb("b_hi", [P, D], F32R)
        b_lo = sb("b_lo", [P, D], F32R)
        a_nat = sb("a_nat", [P, D])
        b_nat = sb("b_nat", [P, NC, ADAPTERS * RANK])

        x_in = sb("x_in", [P, TILES, D])
        xT_hi = sb("xT_hi", [P, NC, PT], F32R)
        xT_lo = sb("xT_lo", [P, NC, PT], F32R)
        xa = sb("xa", [P, PT])
        xa_hi = sb("xa_hi", [P, PT], F32R)
        xa_lo = sb("xa_lo", [P, PT], F32R)
        x0 = sb("x0", [P, TILES, D])
        x1T = sb("x1T", [P, NC, PT])
        x1T_hi = sb("x1T_hi", [P, NC, PT], F32R)
        x1T_lo = sb("x1T_lo", [P, NC, PT], F32R)
        q_bd = sb("q_bd", [P, TILES, HP, P])
        k_bd = sb("k_bd", [P, TILES, HP, P])
        v_bd = sb("v_bd", [P, TILES, SEQT, HP, 2 * HD])
        probs = sb("probs", [P, TILES, HEADS * S])
        row_max = sb("row_max", [P, TILES, HEADS])
        row_sum = sb("row_sum", [P, TILES, HEADS])
        row_inv = sb("row_inv", [P, TILES, HEADS])
        probsT = sb("probsT", [P, TILES, HP * P])
        attnT_hi = sb("attnT_hi", [P, NC, PT], F32R)
        attnT_lo = sb("attnT_lo", [P, NC, PT], F32R)
        x2_hi = sb("x2_hi", [P, TILES, D], F32R)
        x2_lo = sb("x2_lo", [P, TILES, D], F32R)
        y = sb("y", [P, TILES, D])
        w1_in = sb("w1_in", [P, TILES, P])
        w3_in = sb("w3_in", [P, TILES, P])
        w1_bd = sb("w1_bd", [P, TILES, P])
        w3_bd = sb("w3_bd", [P, TILES, P])
        w3_hi = sb("w3_hi", [P, TILES, P], F32R)
        w3_lo = sb("w3_lo", [P, TILES, P], F32R)
        stage = [probsT[:].rearrange("p t (c d) -> p (t c) d", d=D),
                 probs[:].rearrange("p t (c d) -> p (t c) d", d=D),
                 sb("stage2", [P, NC, D])[:]]

        banks = ctx.enter_context(nc.psum_tensor("banks", [P, 8 * BANK], F32))
        bank = [banks[:, b * BANK:(b + 1) * BANK] for b in range(8)]
        banks_23 = banks[:, 2 * BANK:4 * BANK]
        banks_56 = banks[:, 5 * BANK:7 * BANK]

        small_loaded = sem("small_loaded")
        ab_loaded = sem("ab_loaded")
        w_loaded = [sem(f"w_loaded{k}") for k in range(NW)]
        x_loaded = sem("x_loaded")
        w1_loaded = sem("w1_loaded")
        w3_loaded = sem("w3_loaded")
        y_stored = sem("y_stored")
        consts_step = sem("consts_step")
        w_in_zeroed = sem("w_in_zeroed")
        zeroed = sem("zeroed")
        turned = sem("turned")
        turned_hi = sem("turned_hi")
        turned_lo = sem("turned_lo")
        tables_step = sem("tables_step")
        tables_done = sem("tables_done")
        xT_mm = sem("xT_mm")
        xa_mm = sem("xa_mm")
        x0_mm = sem("x0_mm")
        x1_mm = sem("x1_mm")
        k_mm = sem("k_mm")
        q_mm = sem("q_mm")
        v_mm = sem("v_mm")
        s_mm = sem("s_mm")
        pT_mm = sem("pT_mm")
        av_mm = sem("av_mm")
        x2_mm = sem("x2_mm")
        y_mm = sem("y_mm")
        xT_hi_done = sem("xT_hi_done")
        xT_split = sem("xT_split")
        xa_scaled = sem("xa_scaled")
        xa_hi_done = sem("xa_hi_done")
        xa_split = sem("xa_split")
        x0_done = sem("x0_done")
        x1T_done = sem("x1T_done")
        x1_hi_done = sem("x1_hi_done")
        x1_split = sem("x1_split")
        k_placed_act = sem("k_placed_act")
        k_placed_dve = sem("k_placed_dve")
        q_placed_act = sem("q_placed_act")
        q_placed_dve = sem("q_placed_dve")
        v_placed_act = sem("v_placed_act")
        v_placed_dve = sem("v_placed_dve")
        s_masked = sem("s_masked")
        s_max = sem("s_max")
        s_less_max = sem("s_less_max")
        exp_done = sem("exp_done")
        sum_done = sem("sum_done")
        inv_done = sem("inv_done")
        probs_done = sem("probs_done")
        pT_copied_act = sem("pT_copied_act")
        pT_copied_dve = sem("pT_copied_dve")
        attn_hi_done = sem("attn_hi_done")
        attn_split = sem("attn_split")
        x2_hi_done = sem("x2_hi_done")
        x2_split = sem("x2_split")
        y_copied = sem("y_copied")
        w1_ready = sem("w1_ready")
        w3_added = sem("w3_added")
        w3_hi_done = sem("w3_hi_done")
        w3_ready = sem("w3_ready")

        SMALL_DMAS = 3
        AB_DMAS = 1 + NC
        GROUPS_BEFORE_PAIR0 = NC + 2
        GROUPS = NW * NC + 2

        def bank_of_group(g):
            return bank[3 + g % 4]

        def heads(ap):
            return ap.rearrange("p (h k) -> p h k", k=S)

        def tok(t):
            return slice(t * P, (t + 1) * P)

        def half(b):
            return slice(b * 64, (b + 1) * 64)

        def place_k(copy, r, h, b):
            row = r * 64 + h * HD
            src = banks_56[row:row + HD, :].rearrange("p (m t b s) -> p b t m s", m=NC, t=TILES, b=SEQT)[:, b]
            return copy(k_bd[b * 64 + h * HD:b * 64 + (h + 1) * HD, :, r::2, h * S:(h + 1) * S], src)

        def place_q(copy, r, b):
            src = banks_23[half(r), :].rearrange("p (m t b s) -> p b t m s", m=NC, t=TILES, b=SEQT)[:, b]
            return copy(q_bd[half(b), :, r::2, b * S:(b + 1) * S], src)

        def place_v(copy, t, b, h):
            src = bank[4 if t == 0 else 1][half(b), :].rearrange("p (m h e) -> p h m e", h=2, e=HD)[:, h]
            return copy(v_bd[half(h), t, b, :, h * HD:(h + 1) * HD], src)

        block = ctx.enter_context(nc.Block())

        @block.sync
        def _(sp):
            for counted_from_one in (y_copied, y_stored, w3_added, y_mm):
                sp.sem_inc(counted_from_one, 1)
            sp.dma_start(idx1_row[:], idx1.rearrange("(a n) -> a n", a=1)).then_inc(w1_loaded, 16)
            sp.dma_start(idx3_row[:], idx3.rearrange("(a n) -> a n", a=1)).then_inc(w3_loaded, 16)
            sp.dma_start(stage[0], W.rearrange("(c p) d -> p c d", p=P)).then_inc(w_loaded[0], 16)
            sp.dma_start(x_in[:], x_v[0]).then_inc(x_loaded, 16)
            sp.dma_start(a_nat[:], A.rearrange("n r d -> (n r) d")).then_inc(ab_loaded, 16)
            for c in range(NC):
                sp.dma_start(b_nat[:, c, :].rearrange("p (n r) -> p n r", r=RANK),
                             Bm[:, c * P:(c + 1) * P, :].rearrange("n p r -> p n r")).then_inc(ab_loaded, 16)
            sp.dma_start(idx0_all[:], idx0.partition_broadcast(P)).then_inc(small_loaded, 16)
            sp.dma_start(cond_all[:], cond.rearrange("n a -> (n a)").partition_broadcast(P)).then_inc(small_loaded, 16)
            sp.dma_start(scal_of_row[:], scal.rearrange("(n a) -> n a", a=1).to_broadcast([ADAPTERS, RANK]))\
                .then_inc(small_loaded, 16)
            for k in (1, 2):
                sp.dma_start(stage[k], weights[LOADED[k]].rearrange("(c p) d -> p c d", p=P))\
                    .then_inc(w_loaded[k], 16)

            def gather(dst, table, row, rows, arrived, i):
                for t in range(TILES):
                    for b in range(SEQT):
                        at = sp.value_load(row[0:1, bass.ds(i * PSEQ + t * SEQT + b, 1)], min_val=0, max_val=rows - 1)
                        sp.dma_start(dst[half(b), t, half(b)], table[bass.ds(at, 1), :, :].rearrange("a c e -> (a c) e"))\
                            .then_inc(arrived, 16)

            sp.wait_ge(w_in_zeroed, 2)
            sp.wait_ge(w1_loaded, 16)
            sp.wait_ge(w3_loaded, 16)
            gather(w1_in, w1, idx1_row, w1.shape[0], w1_loaded, 0)
            for k in (3, 4):
                sp.wait_ge(turned, GROUPS_BEFORE_PAIR0 + (k - 3) * NC)
                sp.dma_start(stage[k % STAGES], weights[LOADED[k]].rearrange("(c p) d -> p c d", p=P))\
                    .then_inc(w_loaded[k], 16)
            sp.wait_ge(x0_done, TILES)
            sp.dma_start(x_in[:], x_v[1]).then_inc(x_loaded, 16)

            def step(i, next_gather=True, next_x=True):
                if next_gather:
                    sp.wait_ge(w1_ready, i + 1)
                    gather(w1_in, w1, idx1_row, w1.shape[0], w1_loaded, i + 1)
                sp.wait_ge(w3_added, 1 + i)
                gather(w3_in, w3, idx3_row, w3.shape[0], w3_loaded, i)
                if next_x:
                    sp.wait_ge(x0_done, TILES * (i + 2))
                    sp.dma_start(x_in[:], x_v[i + 2] if isinstance(i, int)
                                 else x_v[bass.ds(i + 2, 1)].rearrange("a p t d -> (a p) t d")).then_inc(x_loaded, 16)
                sp.wait_ge(y_copied, 1 + TILES * (i + 1))
                sp.dma_start(out_v[i] if isinstance(i, int)
                             else out_v[bass.ds(i, 1)].rearrange("a p t d -> (a p) t d"), y[:]).then_inc(y_stored, 16)

            with sp.Fori(0, PAIRS - 2) as i:
                step(i)
            step(PAIRS - 2, next_x=False)
            step(PAIRS - 1, next_gather=False, next_x=False)
            sp.wait_ge(y_stored, 1 + 16 * PAIRS)

        @block.tensor
        def _(pe):
            def turn(g, pieces):
                if g >= 4:
                    pe.wait_ge(turned_lo, g - 3)
                for c, piece in enumerate(pieces):
                    last = nc.tensor.transpose(bank_of_group(g)[:, c * P:(c + 1) * P], piece, ident[:])
                last.then_inc(turned, 1)

            def turn_matrix(k, g):
                pe.wait_ge(w_loaded[k], 16)
                for dc in range(NC):
                    turn(g + dc, [stage[k % STAGES][:, oc, dc * P:(dc + 1) * P] for oc in range(NC)])

            def split_products(out_ap, pairs):
                n = len(pairs)
                for k, (s_hi, s_lo, m_hi, m_lo) in enumerate(pairs):
                    nc.tensor.matmul(out_ap, s_hi, m_hi, start=(k == 0), stop=False)
                    nc.tensor.matmul(out_ap, s_hi, m_lo, start=False, stop=False)
                    last = nc.tensor.matmul(out_ap, s_lo, m_hi, start=False, stop=(k == n - 1))
                return last

            def turn_x(i):
                pe.wait_ge(x_loaded, 16 * (i + 1))
                if not (isinstance(i, int) and i == 0):
                    pe.wait_ge(y_copied, 1 + TILES * (i - 1))
                for t in range(TILES):
                    for c in range(NC):
                        last = nc.tensor.transpose(bank[t][:, c * P:(c + 1) * P],
                                                   x_in[:, t, c * P:(c + 1) * P], ident[:])
                    last.then_inc(xT_mm, 1)

            def adapters_down(i):
                pe.wait_ge(xT_split, TILES * (i + 1))
                split_products(bank[2][:, 0:PT],
                               [(a_hi[:, c, :], a_lo[:, c, :], xT_hi[:, c, :], xT_lo[:, c, :])
                                for c in range(NC)]).then_inc(xa_mm, 1)

            def layer0_dense(i):
                for t in range(TILES):
                    for c in range(NC):
                        nc.tensor.matmul(bank[3 + t][:], xT_hi[:, c, tok(t)], w_hi[:, W0, c, :],
                                         start=(c == 0), stop=False)
                        nc.tensor.matmul(bank[3 + t][:], xT_hi[:, c, tok(t)], w_lo[:, W0, c, :],
                                         start=False, stop=False)
                        nc.tensor.matmul(bank[3 + t][:], xT_lo[:, c, tok(t)], w_hi[:, W0, c, :],
                                         start=False, stop=False)

            def adapters_up(i):
                pe.wait_ge(xa_split, i + 1)
                for t in range(TILES):
                    nc.tensor.matmul(bank[3 + t][:], xa_hi[:, tok(t)], b_hi[:], start=False, stop=False)
                    nc.tensor.matmul(bank[3 + t][:], xa_hi[:, tok(t)], b_lo[:], start=False, stop=False)
                    nc.tensor.matmul(bank[3 + t][:], xa_lo[:, tok(t)], b_hi[:],
                                     start=False, stop=True).then_inc(x0_mm, 1)

            def layer1(i):
                pe.wait_ge(w1_ready, i + 1)
                for t in range(TILES):
                    pe.wait_ge(x0_done, TILES * i + t + 1)
                    for c in range(NC):
                        last = nc.tensor.matmul(bank[(7 + t) % 8][:, c * P:(c + 1) * P],
                                                x0[:, t, c * P:(c + 1) * P], w1_bd[:, t, :],
                                                start=True, stop=True)
                    last.then_inc(x1_mm, 1)

            def project_T(w, first_bank):
                for m in range(NC):
                    last = split_products(
                        bank[first_bank + m // 2][:, (m % 2) * PT:(m % 2 + 1) * PT],
                        [(w_hi[:, w, c, m * P:(m + 1) * P], w_lo[:, w, c, m * P:(m + 1) * P],
                          x1T_hi[:, c, :], x1T_lo[:, c, :]) for c in range(NC)])
                return last

            def keys(i):
                pe.wait_ge(x1_split, TILES * (i + 1))
                project_T(WK, 5).then_inc(k_mm, 1)

            def queries(i):
                pe.wait_ge(y_copied, 1 + TILES * i)
                project_T(WQ, 2).then_inc(q_mm, 1)

            def values(t):
                split_products(bank[4 if t == 0 else 1][:],
                               [(x1T_hi[:, c, tok(t)], x1T_lo[:, c, tok(t)], w_hi[:, WV, c, :], w_lo[:, WV, c, :])
                                for c in range(NC)]).then_inc(v_mm, 1)

            def scores(i, t):
                if t == 0:
                    for placed in (k_placed_act, k_placed_dve, q_placed_act, q_placed_dve):
                        pe.wait_ge(placed, i + 1)
                for hp in range(HP):
                    b = (5 + 2 * t + hp // 4) % 8
                    last = nc.tensor.matmul(bank[b][:, hp % 4 * P:(hp % 4 + 1) * P], q_bd[:, t, hp, :],
                                            k_bd[:, t, hp, :], start=True, stop=True)
                last.then_inc(s_mm, 1)

            def turn_probs(i, t):
                pe.wait_ge(probs_done, TILES * i + t + 1)
                for hp in range(HP):
                    b = (5 + 2 * t + hp // 4) % 8
                    last = nc.tensor.transpose(bank[b][:, hp % 4 * P:(hp % 4 + 1) * P],
                                               probs[:, t, hp * P:(hp + 1) * P], ident[:])
                last.then_inc(pT_mm, 1)

            def attend(i, t):
                pe.wait_ge(pT_copied_act, TILES * i + t + 1)
                pe.wait_ge(pT_copied_dve, TILES * i + t + 1)
                if t == 0:
                    pe.wait_ge(v_placed_act, TILES * (i + 1))
                    pe.wait_ge(v_placed_dve, TILES * (i + 1))
                for hp in range(HP):
                    for b in range(SEQT):
                        at = hp * P + b * S
                        last = nc.tensor.matmul(
                            bank[1 + t][half(hp % 2), hp // 2 * P + b * S:hp // 2 * P + (b + 1) * S],
                            v_bd[:, t, b, hp, :], probsT[:, t, at:at + S], start=True, stop=True)
                last.then_inc(av_mm, 1)

            def layer2_out(i):
                for t in range(TILES):
                    for c in range(NC):
                        nc.tensor.matmul(bank[5 + t][:, c * P:(c + 1) * P], x1T[:, c, tok(t)], ident[:],
                                         is_transpose=True, start=(c == 0), stop=False, skip_group_check=True)
                    pe.wait_ge(attn_split, TILES * i + t + 1)
                    for c in range(NC):
                        for s, m in ((attnT_hi, w_hi), (attnT_hi, w_lo), (attnT_lo, w_hi)):
                            last = nc.tensor.matmul(bank[5 + t][:], s[:, c, tok(t)], m[:, WO, c, :], start=False,
                                                    stop=(c == NC - 1 and s is attnT_lo), skip_group_check=True)
                    last.then_inc(x2_mm, 1)

            def layer3(i):
                pe.wait_ge(w3_ready, i + 1)
                for t in range(TILES):
                    pe.wait_ge(x2_split, TILES * i + t + 1)
                    split_products(bank[1 + t][:],
                                   [(w3_hi[:, t, :], w3_lo[:, t, :], x2_hi[:, t, :], x2_lo[:, t, :])])\
                        .then_inc(y_mm, 1)

            def step(i, more=True):
                if more:
                    turn_x(i + 1)
                queries(i)
                values(0)
                scores(i, 0)
                if more:
                    pe.wait_ge(xT_split, TILES * (i + 2))
                scores(i, 1)
                values(1)
                if more:
                    adapters_down(i + 1)
                    pe.wait_ge(v_placed_act, TILES * i + 1)
                    pe.wait_ge(v_placed_dve, TILES * i + 1)
                    layer0_dense(i + 1)
                turn_probs(i, 0)
                turn_probs(i, 1)
                attend(i, 0)
                if more:
                    pe.wait_ge(xa_scaled, i + 2)
                attend(i, 1)
                if more:
                    adapters_up(i + 1)
                layer2_out(i)
                if more:
                    layer1(i + 1)
                layer3(i)
                if more:
                    keys(i + 1)

            pe.wait_ge(consts_step, 7)
            turn_matrix(0, 0)
            pe.wait_ge(ab_loaded, 16 * AB_DMAS)
            turn(NC, [a_nat[:, c * P:(c + 1) * P] for c in range(NC)])
            turn(NC + 1, [b_nat[:, c, :] for c in range(NC)])
            turn_x(0)
            pe.wait_ge(turned_lo, GROUPS_BEFORE_PAIR0)
            adapters_down(0)
            layer0_dense(0)
            adapters_up(0)
            layer1(0)
            for k in range(1, NW):
                turn_matrix(k, GROUPS_BEFORE_PAIR0 + (k - 1) * NC)
            pe.wait_ge(turned_lo, GROUPS)
            keys(0)
            with pe.Fori(0, PAIRS - 1) as i:
                step(i)
            step(PAIRS - 1, more=False)

        @block.scalar
        def _(act):
            def copy(dst, src):
                return nc.scalar.activation(dst, src, ACT.Copy)

            def take_hi(g, dst):
                act.wait_ge(turned, g + 1)
                copy(dst, bank_of_group(g)[:]).then_inc(turned_hi, 1)

            def x_hi(i):
                for t in range(TILES):
                    act.wait_ge(xT_mm, TILES * i + t + 1)
                    copy(xT_hi[:, :, tok(t)], bank[t][:].rearrange("p (c n) -> p c n", n=P)).then_inc(xT_hi_done, 1)

            def xa_hi_part(i):
                act.wait_ge(xa_scaled, i + 1)
                copy(xa_hi[:], xa[:]).then_inc(xa_hi_done, 1)

            def x1_copy(i):
                for t in range(TILES):
                    act.wait_ge(x1_mm, TILES * i + t + 1)
                    copy(x1T[:, :, tok(t)], bank[(7 + t) % 8][:].rearrange("p (c n) -> p c n", n=P))\
                        .then_inc(x1T_done, 1)

            def place_heads(i):
                act.wait_ge(k_mm, i + 1)
                for h in range(2):
                    for b in range(SEQT):
                        last = place_k(copy, 0, h, b)
                last.then_inc(k_placed_act, 1)

            def place_queries(i):
                act.wait_ge(q_mm, i + 1)
                for b in range(SEQT):
                    last = place_q(copy, 0, b)
                last.then_inc(q_placed_act, 1)

            def place_values(i, t):
                act.wait_ge(v_mm, TILES * i + t + 1)
                for h in range(2):
                    last = place_v(copy, t, 0, h)
                last.then_inc(v_placed_act, 1)

            def exps(i):
                for t in range(TILES):
                    act.wait_ge(s_less_max, TILES * i + t + 1)
                    nc.scalar.activation(probs[:, t, :], probs[:, t, :], ACT.Exp).then_inc(exp_done, 1)

            def step(i, more=True):
                place_heads(i)
                if more:
                    x_hi(i + 1)
                place_queries(i)
                place_values(i, 0)
                act.wait_ge(w3_added, 1 + i + 1)
                copy(w3_hi[:], w3_bd[:]).then_inc(w3_hi_done, 1)
                place_values(i, 1)
                exps(i)
                if more:
                    xa_hi_part(i + 1)
                for t in range(TILES):
                    act.wait_ge(pT_mm, TILES * i + t + 1)
                    copy(probsT[:, t, 0:BANK], bank[(5 + 2 * t) % 8][:]).then_inc(pT_copied_act, 1)
                for t in range(TILES):
                    act.wait_ge(av_mm, TILES * i + t + 1)
                    copy(attnT_hi[:, :, tok(t)], bank[1 + t][:].rearrange("p (c n) -> p c n", n=P))\
                        .then_inc(attn_hi_done, 1)
                for t in range(TILES):
                    act.wait_ge(x2_mm, TILES * i + t + 1)
                    copy(x2_hi[:, t, :], bank[5 + t][:]).then_inc(x2_hi_done, 1)
                if more:
                    x1_copy(i + 1)
                act.wait_ge(y_stored, 1 + 16 * i)
                for t in range(TILES):
                    act.wait_ge(y_mm, 1 + TILES * i + t + 1)
                    copy(y[:, t, :], bank[1 + t][:]).then_inc(y_copied, 1)

            for c in range(NC):
                take_hi(c, w_hi[:, W0, c, :])
            take_hi(NC, a_hi[:].rearrange("p c n -> p (c n)"))
            take_hi(NC + 1, b_hi[:])
            x_hi(0)
            xa_hi_part(0)
            x1_copy(0)
            for k in range(1, NW):
                for c in range(NC):
                    take_hi(GROUPS_BEFORE_PAIR0 + (k - 1) * NC + c, w_hi[:, LOADED[k], c, :])
            act.wait_ge(zeroed, 3)
            with act.Fori(0, PAIRS - 1) as i:
                step(i)
            step(PAIRS - 1, more=False)

        @block.vector
        def _(dve):
            def copy(dst, src):
                return nc.vector.tensor_copy(dst, src)

            def rest(dst, whole, hi):
                return nc.vector.tensor_tensor(dst, whole, hi.bitcast(F32), ALU.subtract)

            def take_lo(g, dst, hi):
                dve.wait_ge(turned_hi, g + 1)
                rest(dst, bank_of_group(g)[:], hi).then_inc(turned_lo, 1)

            def x_lo(i):
                for t in range(TILES):
                    dve.wait_ge(xT_hi_done, TILES * i + t + 1)
                    rest(xT_lo[:, :, tok(t)], bank[t][:].rearrange("p (c n) -> p c n", n=P),
                         xT_hi[:, :, tok(t)]).then_inc(xT_split, 1)

            def scale_xa(i):
                dve.wait_ge(xa_mm, i + 1)
                nc.vector.tensor_tensor(
                    xa[:].rearrange("p (b s) -> p b s", s=S),
                    bank[2][:, 0:PT].rearrange("p (b s) -> p b s", s=S),
                    adapter_scale[:, bass.ds(i * PSEQ, PSEQ)].unsqueeze(2).to_broadcast([P, PSEQ, S]),
                    ALU.mult).then_inc(xa_scaled, 1)

            def add_x(i):
                for t in range(TILES):
                    dve.wait_ge(x0_mm, TILES * i + t + 1)
                    nc.vector.tensor_tensor(x0[:, t, :], bank[3 + t][:], x_in[:, t, :], ALU.add)\
                        .then_inc(x0_done, 1)

            def x1_parts(i):
                for t in range(TILES):
                    dve.wait_ge(x1T_done, TILES * i + t + 1)
                    copy(x1T_hi[:, :, tok(t)], x1T[:, :, tok(t)]).then_inc(x1_hi_done, 1)
                    dve.wait_ge(x1_hi_done, TILES * i + t + 1)
                    rest(x1T_lo[:, :, tok(t)], x1T[:, :, tok(t)], x1T_hi[:, :, tok(t)]).then_inc(x1_split, 1)

            def place_values(i, t):
                dve.wait_ge(v_mm, TILES * i + t + 1)
                for h in range(2):
                    last = place_v(copy, t, 1, h)
                last.then_inc(v_placed_dve, 1)

            def mask_and_max(i, t):
                dve.wait_ge(s_mm, TILES * i + t + 1)
                for n in range(2):
                    last = nc.vector.scalar_tensor_tensor(
                        out=heads(probs[:, t, n * BANK:(n + 1) * BANK]), in0=heads(bank[(5 + 2 * t + n) % 8][:]),
                        scalar=beta[:, bass.ds(i * TILES + t, 1)],
                        in1=mask[:].unsqueeze(1).to_broadcast([P, HEADS // 2, S]), op0=ALU.mult, op1=ALU.add)
                last.then_inc(s_masked, 1)
                dve.wait_ge(s_masked, TILES * i + t + 1)
                nc.vector.tensor_reduce(row_max[:, t, :], heads(probs[:, t, :]), AX.X, ALU.max).then_inc(s_max, 1)

            def sums(i, t):
                dve.wait_ge(exp_done, TILES * i + t + 1)
                nc.vector.tensor_reduce(row_sum[:, t, :], heads(probs[:, t, :]), AX.X, ALU.add).then_inc(sum_done, 1)
                dve.wait_ge(sum_done, TILES * i + t + 1)
                nc.vector.reciprocal(row_inv[:, t, :], row_sum[:, t, :]).then_inc(inv_done, 1)

            def step(i, more=True):
                dve.wait_ge(k_mm, i + 1)
                for h in range(2):
                    for b in range(SEQT):
                        last = place_k(copy, 1, h, b)
                last.then_inc(k_placed_dve, 1)
                if more:
                    x_lo(i + 1)
                dve.wait_ge(q_mm, i + 1)
                for b in range(SEQT):
                    last = place_q(copy, 1, b)
                last.then_inc(q_placed_dve, 1)
                place_values(i, 0)
                mask_and_max(i, 0)
                mask_and_max(i, 1)
                place_values(i, 1)
                sums(i, 0)
                if more:
                    scale_xa(i + 1)
                sums(i, 1)
                for t in range(TILES):
                    dve.wait_ge(pT_mm, TILES * i + t + 1)
                    copy(probsT[:, t, BANK:2 * BANK], bank[(6 + 2 * t) % 8][:]).then_inc(pT_copied_dve, 1)
                for t in range(TILES):
                    dve.wait_ge(attn_hi_done, TILES * i + t + 1)
                    rest(attnT_lo[:, :, tok(t)], bank[1 + t][:].rearrange("p (c n) -> p c n", n=P),
                         attnT_hi[:, :, tok(t)]).then_inc(attn_split, 1)
                if more:
                    add_x(i + 1)
                for t in range(TILES):
                    dve.wait_ge(x2_hi_done, TILES * i + t + 1)
                    rest(x2_lo[:, t, :], bank[5 + t][:], x2_hi[:, t, :]).then_inc(x2_split, 1)
                if more:
                    x1_parts(i + 1)

            dve.wait_ge(small_loaded, 16 * SMALL_DMAS)
            dve.wait_ge(consts_step, 7)
            nc.vector.tensor_copy(idx0_f[:], idx0_all[:]).then_inc(tables_step, 1)
            nc.vector.tensor_single_scalar(adapter_of_row[:], row_number[:], int(math.log2(RANK)),
                                           ALU.arith_shift_right).then_inc(tables_step, 1)
            for b in range(SEQT):
                nc.vector.tensor_scalar(beta[half(b), :], cond_all[half(b), b::SEQT], BETA_MAX,
                                        1.0 / math.sqrt(HD), ALU.min, ALU.mult).then_inc(tables_step, 1)
            dve.wait_ge(tables_step, 2 + SEQT)
            nc.vector.tensor_copy(adapter_of_row_f[:], adapter_of_row[:]).then_inc(tables_step, 1)
            dve.wait_ge(tables_step, 3 + SEQT)
            nc.vector.tensor_scalar(adapter_scale[:], idx0_f[:], adapter_of_row_f[:, 0:1], scal_of_row[:, 0:1],
                                    ALU.is_equal, ALU.mult).then_inc(tables_done, 1)
            dve.wait_ge(tables_done, 1)
            for c in range(NC):
                take_lo(c, w_lo[:, W0, c, :], w_hi[:, W0, c, :])
            take_lo(NC, a_lo[:].rearrange("p c n -> p (c n)"), a_hi[:].rearrange("p c n -> p (c n)"))
            take_lo(NC + 1, b_lo[:], b_hi[:])
            x_lo(0)
            scale_xa(0)
            add_x(0)
            x1_parts(0)
            for k in range(1, NW):
                for c in range(NC):
                    w = LOADED[k]
                    take_lo(GROUPS_BEFORE_PAIR0 + (k - 1) * NC + c, w_lo[:, w, c, :], w_hi[:, w, c, :])
            dve.wait_ge(zeroed, 3)
            with dve.Fori(0, PAIRS - 1) as i:
                step(i)
            step(PAIRS - 1, more=False)

        @block.gpsimd
        def _(pool):
            def xa_lo_part(i):
                pool.wait_ge(xa_hi_done, i + 1)
                nc.gpsimd.tensor_tensor(xa_lo[:], xa[:], xa_hi[:].bitcast(F32), ALU.subtract).then_inc(xa_split, 1)

            def add_identity(dst, src):
                return nc.gpsimd.tensor_tensor(dst[:], src[:], ident[:].unsqueeze(1).to_broadcast([P, TILES, P]),
                                               ALU.add)

            def build_w1(i):
                if not (isinstance(i, int) and i == 0):
                    pool.wait_ge(x1_mm, TILES * i)
                pool.wait_ge(w1_loaded, 16 * (1 + PSEQ) + 16 * PSEQ * i)
                add_identity(w1_bd, w1_in).then_inc(w1_ready, 1)

            def build_w3(i):
                pool.wait_ge(y_mm, 1 + TILES * i)
                pool.wait_ge(w3_loaded, 16 * (1 + PSEQ) + 16 * PSEQ * i)
                add_identity(w3_bd, w3_in).then_inc(w3_added, 1)

            def w3_lo_part(i):
                pool.wait_ge(w3_hi_done, i + 1)
                nc.gpsimd.tensor_tensor(w3_lo[:], w3_bd[:], w3_hi[:].bitcast(F32), ALU.subtract).then_inc(w3_ready, 1)

            def with_rows(op, t, rows, done):
                nc.gpsimd.tensor_tensor(heads(probs[:, t, :]), heads(probs[:, t, :]),
                                        rows[:, t, :].unsqueeze(2).to_broadcast([P, HEADS, S]), op).then_inc(done, 1)

            def step(i, more=True):
                build_w3(i)
                if more:
                    build_w1(i + 1)
                for t in range(TILES):
                    pool.wait_ge(s_max, TILES * i + t + 1)
                    with_rows(ALU.subtract, t, row_max, s_less_max)
                for t in range(TILES):
                    pool.wait_ge(inv_done, TILES * i + t + 1)
                    with_rows(ALU.mult, t, row_inv, probs_done)
                if more:
                    xa_lo_part(i + 1)
                w3_lo_part(i)

            nc.gpsimd.memset(ident[:], 0.0).then_inc(consts_step, 1)
            nc.gpsimd.memset(block_mask[:], 0.0).then_inc(consts_step, 1)
            nc.gpsimd.iota(row_number[:], pattern=[[0, 1]], base=0, channel_multiplier=1).then_inc(consts_step, 1)
            pool.wait_ge(consts_step, 3)
            nc.gpsimd.affine_select(out=ident[:], in_=ident[:], compare_op=ALU.not_equal, fill=1.0, base=0,
                                    pattern=[[-1, P]], channel_multiplier=1).then_inc(consts_step, 1)
            nc.gpsimd.affine_select(out=block_mask[:], in_=block_mask[:], compare_op=ALU.is_ge, fill=MASKED, base=0,
                                    pattern=[[-1, P]], channel_multiplier=1).then_inc(consts_step, 1)
            pool.wait_ge(consts_step, 5)
            for b in range(SEQT):
                nc.gpsimd.tensor_copy(mask[half(b), :], block_mask[half(b), half(b)]).then_inc(consts_step, 1)
                pool.wait_ge(consts_step, 6 + b)
            nc.gpsimd.memset(w1_in[:], 0.0).then_inc(w_in_zeroed, 1)
            nc.gpsimd.memset(w3_in[:], 0.0).then_inc(w_in_zeroed, 1)
            for blocks in (k_bd, q_bd, v_bd):
                nc.gpsimd.memset(blocks[:], 0.0).then_inc(zeroed, 1)
            build_w1(0)
            xa_lo_part(0)
            with pool.Fori(0, PAIRS - 1) as i:
                step(i)
            step(PAIRS - 1, more=False)


_INS = ['x', 'itok_B_0_6', 'itok_B_1_198', 'cond_1', 'itok_B_0_7', 'L0_cond_W', 'L0_cond_A', 'L0_cond_Bm',
        'L0_cond_scalings', 'L1_cond_weights', 'L2_cond_Wq', 'L2_cond_Wk', 'L2_cond_Wv', 'L2_cond_Wo',
        'L3_cond_weights']
_OUTS = [((64, 64, 512), 'float32')]


def kernel(**inputs):
    import numpy as _np
    import concourse.bacc as _bacc
    from concourse import mybir as _mybir
    from concourse.bass_utils import run_bass_kernel_spmd as _run

    nc = _bacc.Bacc("TRN2", target_bir_lowering=False, num_devices=1)
    arrays, args = {}, []
    for name in _INS:
        a = _np.ascontiguousarray(inputs[name])
        arrays[f"in_{name}_dram"] = a
        args.append(nc.dram_tensor(f"in_{name}_dram", a.shape, _mybir.dt.from_np(a.dtype), kind="ExternalInput").ap())
    for i, (shape, dtype) in enumerate(_OUTS):
        dt = _mybir.dt.from_np(_np.dtype(dtype))
        args.append(nc.dram_tensor(f"out_{i}_dram", shape, dt, kind="ExternalOutput").ap())
    cond_resid_kernel(nc, *args)
    r = _run(nc, [arrays], core_ids=[0])
    got = tuple(r.results[0][f"out_{i}_dram"] for i in range(len(_OUTS)))
    return got[0]
```

```python
import math
from contextlib import ExitStack

import concourse.bass as bass
from concourse import mybir

F32 = mybir.dt.float32
F32R = mybir.dt.float32r
I32 = mybir.dt.int32
ALU = mybir.AluOpType
ACT = mybir.ActivationFunctionType
AX = mybir.AxisListType

P = 128
SEQS, S, D = 64, 64, 512
NC = D // P
TILES = 2
PT = TILES * P
PAIRS = SEQS * S // PT
PSEQ = PT // S
SEQT = P // S
HEADS, HD = 16, 32
HP = HEADS // 2
ADAPTERS, RANK = 8, 16
MASKED = -1.0e30
BETA_MAX = 4.0
BANK = 512
NW = 5
W0, WQ, WK, WV, WO = range(NW)
LOADED = (W0, WK, WQ, WV, WO)
STAGES = 3


def cond_resid_kernel(nc, x, idx0, idx1, cond, idx3, W, A, Bm, scal, w1, Wq, Wk, Wv, Wo, w3, out):
    weights = {W0: W, WQ: Wq, WK: Wk, WV: Wv, WO: Wo}
    x_v = x.rearrange("(i t b) s d -> i (b s) t d", t=TILES, b=SEQT)
    out_v = out.rearrange("(i t b) s d -> i (b s) t d", t=TILES, b=SEQT)

    b_parts = nc.dram_tensor("b_parts", [2, ADAPTERS * RANK, D], F32, kind="Internal").ap()

    with ExitStack() as ctx:
        def sb(name, shape, dt=F32):
            return ctx.enter_context(nc.sbuf_tensor(name, shape, dt))

        def sem(name):
            return ctx.enter_context(nc.semaphore(name))

        ctx.enter_context(nc.allow_non_contiguous_dma(reason="a few small tables are loaded once"))

        ident = sb("ident", [P, P])
        mask = sb("mask", [P, S])
        block_mask = sb("block_mask", [P, P])
        idx0_row = sb("idx0_row", [1, SEQS], I32)
        idx0_all = sb("idx0_all", [P, SEQS], I32)
        idx0_f = sb("idx0_f", [P, SEQS])
        scal_all = sb("scal_all", [P, ADAPTERS])
        scal_of = sb("scal_of", [P, ADAPTERS, SEQS])
        scal_sum = sb("scal_sum", [P, SEQS])
        own_rows = sb("own_rows", [PSEQ * RANK, PSEQ])
        scal_rows = sb("scal_rows", [PSEQ * RANK, PAIRS, PSEQ])
        idx1_row = sb("idx1_row", [1, SEQS], I32)
        idx3_row = sb("idx3_row", [1, SEQS], I32)
        cond_all = sb("cond_all", [P, SEQS])
        beta = sb("beta", [P, PAIRS * TILES])
        w_hi = sb("w_hi", [P, NW, NC, D], F32R)
        w_lo = sb("w_lo", [P, NW, NC, D], F32R)
        a_all = sb("a_all", [P, NC, 2, P], F32R)
        b_hi = sb("b_hi", [P, D], F32R)
        b_lo = sb("b_lo", [P, D], F32R)

        x_in = sb("x_in", [P, TILES, D])
        xT_hi = sb("xT_hi", [P, NC, PT], F32R)
        xT_lo = sb("xT_lo", [P, NC, PT], F32R)
        a_sel = sb("a_sel", [P, NC, 2, PSEQ * RANK], F32R)
        b_sel = sb("b_sel", [3 * SEQT * RANK, TILES, D], F32R)
        xa_low = sb("xa_low", [PSEQ * RANK, PT])
        xa_sum = sb("xa_sum", [PSEQ * RANK, PT])
        xa = sb("xa", [PSEQ * RANK, PT])
        xa_hi = sb("xa_hi", [PSEQ * RANK, PT], F32R)
        xa_parts = sb("xa_parts", [3 * SEQT * RANK, TILES, P], F32R)
        x0 = sb("x0", [P, TILES, D])
        x1T = sb("x1T", [P, NC, PT])
        x1T_hi = sb("x1T_hi", [P, NC, PT], F32R)
        x1T_lo = sb("x1T_lo", [P, NC, PT], F32R)
        q_bd = sb("q_bd", [P, TILES, HP, P])
        k_bd = sb("k_bd", [P, TILES, HP, P])
        v_bd = sb("v_bd", [P, TILES, SEQT, HP, 2 * HD])
        probs = sb("probs", [P, TILES, HEADS * S])
        row_max = sb("row_max", [P, TILES, HEADS])
        row_sum = sb("row_sum", [P, TILES, HEADS])
        row_inv = sb("row_inv", [P, TILES, HEADS])
        probsT = sb("probsT", [P, TILES, HP * P])
        attnT_hi = sb("attnT_hi", [P, NC, PT], F32R)
        attnT_lo = sb("attnT_lo", [P, NC, PT], F32R)
        x2_hi = sb("x2_hi", [P, TILES, D], F32R)
        x2_lo = sb("x2_lo", [P, TILES, D], F32R)
        y = sb("y", [P, TILES, D])
        w1_in = sb("w1_in", [P, TILES, P])
        w3_in = sb("w3_in", [P, TILES, P])
        w1_bd = sb("w1_bd", [P, TILES, P])
        w3_bd = sb("w3_bd", [P, TILES, P])
        w3_hi = sb("w3_hi", [P, TILES, P], F32R)
        w3_lo = sb("w3_lo", [P, TILES, P], F32R)
        a_nat = y[:, 0, :]
        b_nat = y[:, 1, :].rearrange("p (c n) -> p c n", c=NC)
        stage = [probsT[:].rearrange("p t (c d) -> p (t c) d", d=D),
                 probs[:].rearrange("p t (c d) -> p (t c) d", d=D),
                 sb("stage2", [P, NC, D])[:]]

        banks = ctx.enter_context(nc.psum_tensor("banks", [P, 8 * BANK], F32))
        bank = [banks[:, b * BANK:(b + 1) * BANK] for b in range(8)]
        banks_23 = banks[:, 2 * BANK:4 * BANK]
        banks_56 = banks[:, 5 * BANK:7 * BANK]

        small_loaded = sem("small_loaded")
        ab_loaded = sem("ab_loaded")
        w_loaded = [sem(f"w_loaded{k}") for k in range(NW)]
        x_loaded = sem("x_loaded")
        b_parts_stored = sem("b_parts_stored")
        b_loaded = sem("b_loaded")
        w1_loaded = sem("w1_loaded")
        w3_loaded = sem("w3_loaded")
        y_stored = sem("y_stored")
        consts_step = sem("consts_step")
        w_in_zeroed = sem("w_in_zeroed")
        zeroed = sem("zeroed")
        turned = sem("turned")
        turned_hi = sem("turned_hi")
        turned_lo = sem("turned_lo")
        tables_step = sem("tables_step")
        tables_done = sem("tables_done")
        xT_mm = sem("xT_mm")
        xa_mm = sem("xa_mm")
        x0_mm = sem("x0_mm")
        x1_mm = sem("x1_mm")
        k_mm = sem("k_mm")
        q_mm = sem("q_mm")
        v_mm = sem("v_mm")
        s_mm = sem("s_mm")
        pT_mm = sem("pT_mm")
        av_mm = sem("av_mm")
        x2_mm = sem("x2_mm")
        y_mm = sem("y_mm")
        xT_hi_done = sem("xT_hi_done")
        xT_split = sem("xT_split")
        a_ready = sem("a_ready")
        xa_low_done = sem("xa_low_done")
        xa_summed = sem("xa_summed")
        xa_scaled = sem("xa_scaled")
        xa_hi_done = sem("xa_hi_done")
        xa_hi_placed = sem("xa_hi_placed")
        xa_lo_placed = sem("xa_lo_placed")
        x0_done = sem("x0_done")
        x1T_done = sem("x1T_done")
        x1_hi_done = sem("x1_hi_done")
        x1_split = sem("x1_split")
        k_placed_act = sem("k_placed_act")
        k_placed_dve = sem("k_placed_dve")
        q_placed_act = sem("q_placed_act")
        q_placed_dve = sem("q_placed_dve")
        v_placed = sem("v_placed")
        s_masked = sem("s_masked")
        s_max = sem("s_max")
        s_less_max = sem("s_less_max")
        exp_done = sem("exp_done")
        sum_done = sem("sum_done")
        inv_done = sem("inv_done")
        probs_done = sem("probs_done")
        pT_copied_act = sem("pT_copied_act")
        pT_copied_dve = sem("pT_copied_dve")
        attn_hi_done = sem("attn_hi_done")
        attn_split = sem("attn_split")
        x2_hi_done = sem("x2_hi_done")
        x2_split = sem("x2_split")
        y_copied = sem("y_copied")
        w1_ready = sem("w1_ready")
        w3_added = sem("w3_added")
        w3_hi_done = sem("w3_hi_done")
        w3_ready = sem("w3_ready")

        SMALL_DMAS = 4
        AB_DMAS = 1 + NC
        GROUPS_BEFORE_PAIR0 = NC + 2
        GROUPS = NW * NC + 2

        ring = [3 + g % 4 for g in range(GROUPS_BEFORE_PAIR0)]
        ring += [5 + g % 3 for g in range(GROUPS - GROUPS_BEFORE_PAIR0)]

        def bank_of_group(g):
            return bank[ring[g]]

        def groups_of(k):
            first = GROUPS_BEFORE_PAIR0 + (k - 1) * NC
            return range(first, first + NC)

        def heads(ap):
            return ap.rearrange("p (h k) -> p h k", k=S)

        def tok(t):
            return slice(t * P, (t + 1) * P)

        def half(b):
            return slice(b * 64, (b + 1) * 64)

        def place_k(copy, r, h, b):
            row = r * 64 + h * HD
            src = banks_56[row:row + HD, :].rearrange("p (m t b s) -> p b t m s", m=NC, t=TILES, b=SEQT)[:, b]
            return copy(k_bd[b * 64 + h * HD:b * 64 + (h + 1) * HD, :, r::2, h * S:(h + 1) * S], src)

        def place_q(copy, r, b):
            src = banks_23[half(r), :].rearrange("p (m t b s) -> p b t m s", m=NC, t=TILES, b=SEQT)[:, b]
            return copy(q_bd[half(b), :, r::2, b * S:(b + 1) * S], src)

        def place_v(copy, t, b, h):
            src = bank[4 if t == 0 else 1][half(b), :].rearrange("p (m h e) -> p h m e", h=2, e=HD)[:, h]
            return copy(v_bd[half(h), t, b, :, h * HD:(h + 1) * HD], src)

        block = ctx.enter_context(nc.Block())

        @block.sync
        def _(sp):
            for counted_from_one in (y_copied, y_stored, w3_added, y_mm):
                sp.sem_inc(counted_from_one, 1)
            sp.dma_start(x_in[:], x_v[0]).then_inc(x_loaded, 16)
            sp.dma_start(stage[0], W.rearrange("(c p) d -> p c d", p=P)).then_inc(w_loaded[0], 16)
            sp.dma_start(a_nat, A.rearrange("n r d -> (n r) d")).then_inc(ab_loaded, 16)
            for c in range(NC):
                sp.dma_start(b_nat[:, c, :].rearrange("p (n r) -> p n r", r=RANK),
                             Bm[:, c * P:(c + 1) * P, :].rearrange("n p r -> p n r")).then_inc(ab_loaded, 16)
            sp.dma_start(idx1_row[:], idx1.rearrange("(a n) -> a n", a=1)).then_inc(w1_loaded, 16)
            sp.dma_start(idx3_row[:], idx3.rearrange("(a n) -> a n", a=1)).then_inc(w3_loaded, 16)
            sp.dma_start(idx0_row[:], idx0.rearrange("(a n) -> a n", a=1)).then_inc(small_loaded, 16)
            sp.dma_start(idx0_all[:], idx0.partition_broadcast(P)).then_inc(small_loaded, 16)
            sp.dma_start(cond_all[:], cond.rearrange("n a -> (n a)").partition_broadcast(P)).then_inc(small_loaded, 16)
            sp.dma_start(scal_all[:], scal.partition_broadcast(P)).then_inc(small_loaded, 16)
            for k in (1, 2):
                sp.dma_start(stage[k], weights[LOADED[k]].rearrange("(c p) d -> p c d", p=P))\
                    .then_inc(w_loaded[k], 16)

            def pair_indices(row, rows, i):
                return [sp.value_load(row[0:1, bass.ds(i * PSEQ + n, 1)], min_val=0, max_val=rows - 1)
                        for n in range(PSEQ)]

            def gather(dst, table, at, arrived):
                for n in range(PSEQ):
                    t, b = divmod(n, SEQT)
                    sp.dma_start(dst[half(b), t, half(b)], table[bass.ds(at[n], 1), :, :].rearrange("a c e -> (a c) e"))\
                        .then_inc(arrived, 16)

            def gather_b(at):
                for n in range(PSEQ):
                    t, b = divmod(n, SEQT)
                    for k, part in enumerate((0, 0, 1)):
                        row = (k * SEQT + b) * RANK
                        sp.dma_start(b_sel[row:row + RANK, t, :].bitcast(F32),
                                     b_parts[part, bass.ds(at[n] * RANK, RANK), :]).then_inc(b_loaded, 16)

            sp.wait_ge(w_in_zeroed, 2)
            sp.wait_ge(w1_loaded, 16)
            sp.wait_ge(w3_loaded, 16)
            gather(w1_in, w1, pair_indices(idx1_row, w1.shape[0], 0), w1_loaded)
            gather(w3_in, w3, pair_indices(idx3_row, w3.shape[0], 0), w3_loaded)
            sp.wait_ge(turned_lo, GROUPS_BEFORE_PAIR0)
            for part, b_part in enumerate((b_hi, b_lo)):
                sp.dma_start(b_parts[part], b_part[:].bitcast(F32)).then_inc(b_parts_stored, 16)
            sp.wait_ge(small_loaded, 16 * SMALL_DMAS)
            sp.wait_ge(b_parts_stored, 16 * 2)
            gather_b(pair_indices(idx0_row, ADAPTERS, 0))
            for k in (3, 4):
                sp.wait_ge(turned, GROUPS_BEFORE_PAIR0 + (k - 3) * NC)
                sp.dma_start(stage[k % STAGES], weights[LOADED[k]].rearrange("(c p) d -> p c d", p=P))\
                    .then_inc(w_loaded[k], 16)
            sp.wait_ge(x0_done, TILES)
            sp.dma_start(x_in[:], x_v[1]).then_inc(x_loaded, 16)
            gather_b(pair_indices(idx0_row, ADAPTERS, 1))

            def step(i, left):
                if left >= 1:
                    at1 = pair_indices(idx1_row, w1.shape[0], i + 1)
                    at3 = pair_indices(idx3_row, w3.shape[0], i + 1)
                    sp.wait_ge(w1_ready, i + 1)
                    gather(w1_in, w1, at1, w1_loaded)
                    sp.wait_ge(w3_added, 1 + (i + 1))
                    gather(w3_in, w3, at3, w3_loaded)
                if left >= 2:
                    at0 = pair_indices(idx0_row, ADAPTERS, i + 2)
                    sp.wait_ge(x0_done, TILES * (i + 2))
                    sp.dma_start(x_in[:], x_v[i + 2] if isinstance(i, int)
                                 else x_v[bass.ds(i + 2, 1)].rearrange("a p t d -> (a p) t d")).then_inc(x_loaded, 16)
                    gather_b(at0)
                sp.wait_ge(y_copied, 1 + TILES * (i + 1))
                sp.dma_start(out_v[i] if isinstance(i, int)
                             else out_v[bass.ds(i, 1)].rearrange("a p t d -> (a p) t d"), y[:]).then_inc(y_stored, 16)

            with sp.Fori(0, PAIRS - 2) as i:
                step(i, 2)
            step(PAIRS - 2, 1)
            step(PAIRS - 1, 0)
            sp.wait_ge(y_stored, 1 + 16 * PAIRS)

        @block.tensor
        def _(pe):
            def turn(g, pieces):
                before = [n for n in range(g) if ring[n] == ring[g]]
                if before:
                    pe.wait_ge(turned_lo, before[-1] + 1)
                for c, piece in enumerate(pieces):
                    last = nc.tensor.transpose(bank_of_group(g)[:, c * P:(c + 1) * P], piece, ident[:])
                last.then_inc(turned, 1)

            def turn_matrix(k, g):
                pe.wait_ge(w_loaded[k], 16)
                for dc in range(NC):
                    turn(g + dc, [stage[k % STAGES][:, oc, dc * P:(dc + 1) * P] for oc in range(NC)])

            def split_products(out_ap, pairs):
                n = len(pairs)
                for k, (s_hi, s_lo, m_hi, m_lo) in enumerate(pairs):
                    nc.tensor.matmul(out_ap, s_hi, m_hi, start=(k == 0), stop=False)
                    nc.tensor.matmul(out_ap, s_hi, m_lo, start=False, stop=False)
                    last = nc.tensor.matmul(out_ap, s_lo, m_hi, start=False, stop=(k == n - 1))
                return last

            def turn_x(i):
                pe.wait_ge(x_loaded, 16 * (i + 1))
                if not (isinstance(i, int) and i == 0):
                    pe.wait_ge(y_copied, 1 + TILES * (i - 1))
                for t in range(TILES):
                    for c in range(NC):
                        last = nc.tensor.transpose(bank[t][:, c * P:(c + 1) * P],
                                                   x_in[:, t, c * P:(c + 1) * P], ident[:])
                    last.then_inc(xT_mm, 1)

            def adapters_down(i):
                pe.wait_ge(a_ready, i + 1)
                pe.wait_ge(xT_split, TILES * (i + 1))
                for c in range(NC):
                    for part in (xT_hi, xT_lo):
                        last = nc.tensor.matmul(bank[2][:, 0:PT], a_sel[:, c, :, :].rearrange("p a n -> p (a n)"),
                                                part[:, c, :], start=(c == 0 and part is xT_hi),
                                                stop=(c == NC - 1 and part is xT_lo))
                last.then_inc(xa_mm, 1)

            def layer0_dense(i):
                for t in range(TILES):
                    for c in range(NC):
                        nc.tensor.matmul(bank[3 + t][:], xT_hi[:, c, tok(t)], w_hi[:, W0, c, :],
                                         start=(c == 0), stop=False)
                        nc.tensor.matmul(bank[3 + t][:], xT_hi[:, c, tok(t)], w_lo[:, W0, c, :],
                                         start=False, stop=False)
                        nc.tensor.matmul(bank[3 + t][:], xT_lo[:, c, tok(t)], w_hi[:, W0, c, :],
                                         start=False, stop=False)

            def adapters_up(i):
                pe.wait_ge(b_loaded, 16 * 3 * PSEQ * (i + 1))
                pe.wait_ge(xa_hi_placed, i + 1)
                pe.wait_ge(xa_lo_placed, i + 1)
                for t in range(TILES):
                    nc.tensor.matmul(bank[3 + t][:], xa_parts[:, t, :], b_sel[:, t, :],
                                     start=False, stop=True).then_inc(x0_mm, 1)

            def layer1(i):
                pe.wait_ge(w1_ready, i + 1)
                for t in range(TILES):
                    pe.wait_ge(x0_done, TILES * i + t + 1)
                    for c in range(NC):
                        last = nc.tensor.matmul(bank[(7 + t) % 8][:, c * P:(c + 1) * P],
                                                x0[:, t, c * P:(c + 1) * P], w1_bd[:, t, :],
                                                start=True, stop=True)
                    last.then_inc(x1_mm, 1)

            def project_T(w, first_bank, m):
                return split_products(
                    bank[first_bank + m // 2][:, (m % 2) * PT:(m % 2 + 1) * PT],
                    [(w_hi[:, w, c, m * P:(m + 1) * P], w_lo[:, w, c, m * P:(m + 1) * P],
                      x1T_hi[:, c, :], x1T_lo[:, c, :]) for c in range(NC)])

            def keys(i, chunks):
                if chunks[0] == 0:
                    pe.wait_ge(x1_split, TILES * (i + 1))
                for m in chunks:
                    last = project_T(WK, 5, m)
                if chunks[-1] == NC - 1:
                    last.then_inc(k_mm, 1)

            def queries(i):
                pe.wait_ge(y_copied, 1 + TILES * i)
                for m in range(NC):
                    last = project_T(WQ, 2, m)
                last.then_inc(q_mm, 1)

            def values(t):
                split_products(bank[4 if t == 0 else 1][:],
                               [(x1T_hi[:, c, tok(t)], x1T_lo[:, c, tok(t)], w_hi[:, WV, c, :], w_lo[:, WV, c, :])
                                for c in range(NC)]).then_inc(v_mm, 1)

            def scores(i, t):
                if t == 0:
                    for placed in (k_placed_act, k_placed_dve, q_placed_act, q_placed_dve):
                        pe.wait_ge(placed, i + 1)
                for hp in range(HP):
                    b = (5 + 2 * t + hp // 4) % 8
                    last = nc.tensor.matmul(bank[b][:, hp % 4 * P:(hp % 4 + 1) * P], q_bd[:, t, hp, :],
                                            k_bd[:, t, hp, :], start=True, stop=True)
                last.then_inc(s_mm, 1)

            def turn_probs(i, t):
                pe.wait_ge(probs_done, TILES * i + t + 1)
                for hp in range(HP):
                    b = (5 + 2 * t + hp // 4) % 8
                    last = nc.tensor.transpose(bank[b][:, hp % 4 * P:(hp % 4 + 1) * P],
                                               probs[:, t, hp * P:(hp + 1) * P], ident[:])
                last.then_inc(pT_mm, 1)

            def attend(i, t):
                pe.wait_ge(pT_copied_act, TILES * i + t + 1)
                pe.wait_ge(pT_copied_dve, TILES * i + t + 1)
                if t == 0:
                    pe.wait_ge(v_placed, TILES * (i + 1))
                for hp in range(HP):
                    for b in range(SEQT):
                        at = hp * P + b * S
                        last = nc.tensor.matmul(
                            bank[1 + t][half(hp % 2), hp // 2 * P + b * S:hp // 2 * P + (b + 1) * S],
                            v_bd[:, t, b, hp, :], probsT[:, t, at:at + S], start=True, stop=True)
                last.then_inc(av_mm, 1)

            def turn_x1(i):
                for t in range(TILES):
                    for c in range(NC):
                        nc.tensor.matmul(bank[5 + t][:, c * P:(c + 1) * P], x1T[:, c, tok(t)], ident[:],
                                         is_transpose=True, start=(c == 0), stop=False, skip_group_check=True)

            def layer2_out(i, t):
                pe.wait_ge(attn_split, TILES * i + t + 1)
                for c in range(NC):
                    for s, m in ((attnT_hi, w_hi), (attnT_hi, w_lo), (attnT_lo, w_hi)):
                        last = nc.tensor.matmul(bank[5 + t][:], s[:, c, tok(t)], m[:, WO, c, :], start=False,
                                                stop=(c == NC - 1 and s is attnT_lo), skip_group_check=True)
                last.then_inc(x2_mm, 1)

            def layer3(i, t):
                if t == 0:
                    pe.wait_ge(w3_ready, i + 1)
                pe.wait_ge(x2_split, TILES * i + t + 1)
                split_products(bank[1 + t][:],
                               [(w3_hi[:, t, :], w3_lo[:, t, :], x2_hi[:, t, :], x2_lo[:, t, :])]).then_inc(y_mm, 1)

            def step(i, more=True):
                if more:
                    turn_x(i + 1)
                queries(i)
                values(0)
                scores(i, 0)
                if more:
                    pe.wait_ge(xT_split, TILES * (i + 2))
                scores(i, 1)
                values(1)
                if more:
                    adapters_down(i + 1)
                    pe.wait_ge(v_placed, TILES * i + 1)
                    layer0_dense(i + 1)
                turn_probs(i, 0)
                turn_probs(i, 1)
                attend(i, 0)
                if more:
                    pe.wait_ge(xa_summed, i + 2)
                attend(i, 1)
                if more:
                    adapters_up(i + 1)
                turn_x1(i)
                layer2_out(i, 0)
                if more:
                    layer1(i + 1)
                layer2_out(i, 1)
                layer3(i, 0)
                if more:
                    keys(i + 1, [0, 1])
                layer3(i, 1)
                if more:
                    keys(i + 1, [2, 3])

            pe.wait_ge(consts_step, 9)
            turn_x(0)
            turn_matrix(0, 0)
            pe.wait_ge(ab_loaded, 16 * AB_DMAS)
            turn(NC, [a_nat[:, c * P:(c + 1) * P] for c in range(NC)])
            turn(NC + 1, [b_nat[:, c, :] for c in range(NC)])
            turn_matrix(1, groups_of(1)[0])
            adapters_down(0)
            layer0_dense(0)
            turn_matrix(2, groups_of(2)[0])
            adapters_up(0)
            pe.wait_ge(turned_lo, groups_of(2)[-1] + 1)
            layer1(0)
            pe.wait_ge(x1T_done, 1)
            for k in (3, 4):
                turn_matrix(k, groups_of(k)[0])
            pe.wait_ge(turned_lo, GROUPS)
            keys(0, range(NC))
            with pe.Fori(0, PAIRS - 1) as i:
                step(i)
            step(PAIRS - 1, more=False)

        @block.scalar
        def _(act):
            def copy(dst, src):
                return nc.scalar.activation(dst, src, ACT.Copy)

            def take_hi(g, dst, view="p n -> p n"):
                act.wait_ge(turned, g + 1)
                sizes = {"c": NC} if "(" in view else {}
                copy(dst, bank_of_group(g)[:].rearrange(view, **sizes)).then_inc(turned_hi, 1)

            def x_hi(i):
                for t in range(TILES):
                    act.wait_ge(xT_mm, TILES * i + t + 1)
                    copy(xT_hi[:, :, tok(t)], bank[t][:].rearrange("p (c n) -> p c n", n=P)).then_inc(xT_hi_done, 1)

            def select_a(i):
                for n in range(PSEQ):
                    at = act.value_load(idx0_row[0:1, bass.ds(i * PSEQ + n, 1)], min_val=0, max_val=ADAPTERS - 1)
                    last = copy(a_sel[:, :, :, n * RANK:(n + 1) * RANK], a_all[:, :, :, bass.ds(at * RANK, RANK)])
                last.then_inc(a_ready, 1)

            def xa_low_part(i):
                act.wait_ge(xa_mm, i + 1)
                copy(xa_low[:], bank[2][half(1), 0:PT]).then_inc(xa_low_done, 1)

            def xa_hi_part(i):
                act.wait_ge(xa_scaled, i + 1)
                copy(xa_hi[:], xa[:]).then_inc(xa_hi_done, 1)
                act.wait_ge(xa_hi_done, i + 1)
                n = SEQT * RANK
                for t in range(TILES):
                    for part in (0, 2):
                        last = copy(xa_parts[part * n:(part + 1) * n, t, :], xa_hi[t * n:(t + 1) * n, tok(t)])
                last.then_inc(xa_hi_placed, 1)

            def x1_copy(i):
                for t in range(TILES):
                    act.wait_ge(x1_mm, TILES * i + t + 1)
                    copy(x1T[:, :, tok(t)], bank[(7 + t) % 8][:].rearrange("p (c n) -> p c n", n=P))\
                        .then_inc(x1T_done, 1)

            def place_heads(i):
                act.wait_ge(k_mm, i + 1)
                for h in range(2):
                    for b in range(SEQT):
                        last = place_k(copy, 0, h, b)
                last.then_inc(k_placed_act, 1)

            def place_queries(i):
                act.wait_ge(q_mm, i + 1)
                for b in range(SEQT):
                    last = place_q(copy, 0, b)
                last.then_inc(q_placed_act, 1)

            def place_values(i, t):
                act.wait_ge(v_mm, TILES * i + t + 1)
                for b in range(SEQT):
                    for h in range(2):
                        last = place_v(copy, t, b, h)
                last.then_inc(v_placed, 1)

            def exp(i, t):
                act.wait_ge(s_less_max, TILES * i + t + 1)
                nc.scalar.activation(probs[:, t, :], probs[:, t, :], ACT.Exp).then_inc(exp_done, 1)

            def x2_hi_part(i, t):
                act.wait_ge(x2_mm, TILES * i + t + 1)
                copy(x2_hi[:, t, :], bank[5 + t][:]).then_inc(x2_hi_done, 1)

            def step(i, more=True):
                place_heads(i)
                if more:
                    x_hi(i + 1)
                    select_a(i + 1)
                place_queries(i)
                place_values(i, 0)
                act.wait_ge(w3_added, 1 + i + 1)
                copy(w3_hi[:], w3_bd[:]).then_inc(w3_hi_done, 1)
                exp(i, 0)
                if more:
                    xa_low_part(i + 1)
                place_values(i, 1)
                exp(i, 1)
                for t in range(TILES):
                    act.wait_ge(pT_mm, TILES * i + t + 1)
                    copy(probsT[:, t, 0:BANK], bank[(5 + 2 * t) % 8][:]).then_inc(pT_copied_act, 1)
                if more:
                    xa_hi_part(i + 1)
                for t in range(TILES):
                    act.wait_ge(av_mm, TILES * i + t + 1)
                    copy(attnT_hi[:, :, tok(t)], bank[1 + t][:].rearrange("p (c n) -> p c n", n=P))\
                        .then_inc(attn_hi_done, 1)
                x2_hi_part(i, 0)
                if more:
                    x1_copy(i + 1)
                x2_hi_part(i, 1)
                act.wait_ge(y_stored, 1 + 16 * i)
                for t in range(TILES):
                    act.wait_ge(y_mm, 1 + TILES * i + t + 1)
                    copy(y[:, t, :], bank[1 + t][:]).then_inc(y_copied, 1)

            def take_matrix(k):
                for c, g in enumerate(groups_of(k)):
                    take_hi(g, w_hi[:, LOADED[k], c, :])

            x_hi(0)
            for c in range(NC):
                take_hi(c, w_hi[:, W0, c, :])
            take_hi(NC, a_all[:, :, 0, :], "p (c n) -> p c n")
            take_hi(NC + 1, b_hi[:])
            act.wait_ge(turned_lo, GROUPS_BEFORE_PAIR0)
            act.wait_ge(small_loaded, 16 * SMALL_DMAS)
            select_a(0)
            take_matrix(1)
            xa_low_part(0)
            xa_hi_part(0)
            take_matrix(2)
            x1_copy(0)
            take_matrix(3)
            take_matrix(4)
            act.wait_ge(zeroed, 3)
            with act.Fori(0, PAIRS - 1) as i:
                step(i)
            step(PAIRS - 1, more=False)

        @block.vector
        def _(dve):
            def copy(dst, src):
                return nc.vector.tensor_copy(dst, src)

            def rest(dst, whole, hi):
                return nc.vector.tensor_tensor(dst, whole, hi.bitcast(F32), ALU.subtract)

            def take_lo(g, dst, hi, view="p n -> p n"):
                dve.wait_ge(turned_hi, g + 1)
                sizes = {"c": NC} if "(" in view else {}
                rest(dst, bank_of_group(g)[:].rearrange(view, **sizes), hi).then_inc(turned_lo, 1)

            def x_lo(i):
                for t in range(TILES):
                    dve.wait_ge(xT_hi_done, TILES * i + t + 1)
                    rest(xT_lo[:, :, tok(t)], bank[t][:].rearrange("p (c n) -> p c n", n=P),
                         xT_hi[:, :, tok(t)]).then_inc(xT_split, 1)

            def sum_xa(i):
                dve.wait_ge(xa_low_done, i + 1)
                nc.vector.tensor_tensor(xa_sum[:], bank[2][half(0), 0:PT], xa_low[:], ALU.add).then_inc(xa_summed, 1)

            def scale_xa(i):
                dve.wait_ge(xa_summed, i + 1)
                nc.vector.tensor_tensor(
                    xa[:].rearrange("p (b s) -> p b s", s=S), xa_sum[:].rearrange("p (b s) -> p b s", s=S),
                    scal_rows[:, bass.ds(i, 1), :].rearrange("p a b -> p (a b)").unsqueeze(2)
                    .to_broadcast([PSEQ * RANK, PSEQ, S]), ALU.mult).then_inc(xa_scaled, 1)

            def xa_lo_part(i):
                dve.wait_ge(xa_hi_done, i + 1)
                n = SEQT * RANK
                for t in range(TILES):
                    rows = slice(t * n, (t + 1) * n)
                    last = rest(xa_parts[n:2 * n, t, :], xa[rows, tok(t)], xa_hi[rows, tok(t)])
                last.then_inc(xa_lo_placed, 1)

            def add_x(i):
                for t in range(TILES):
                    dve.wait_ge(x0_mm, TILES * i + t + 1)
                    nc.vector.tensor_tensor(x0[:, t, :], bank[3 + t][:], x_in[:, t, :], ALU.add)\
                        .then_inc(x0_done, 1)

            def x1_parts(i):
                for t in range(TILES):
                    dve.wait_ge(x1T_done, TILES * i + t + 1)
                    copy(x1T_hi[:, :, tok(t)], x1T[:, :, tok(t)]).then_inc(x1_hi_done, 1)
                    dve.wait_ge(x1_hi_done, TILES * i + t + 1)
                    rest(x1T_lo[:, :, tok(t)], x1T[:, :, tok(t)], x1T_hi[:, :, tok(t)]).then_inc(x1_split, 1)

            def x2_lo_part(i, t):
                dve.wait_ge(x2_hi_done, TILES * i + t + 1)
                rest(x2_lo[:, t, :], bank[5 + t][:], x2_hi[:, t, :]).then_inc(x2_split, 1)

            def less_max(i, t):
                dve.wait_ge(s_max, TILES * i + t + 1)
                dve.wait_ge(s_less_max, TILES * i + t)
                nc.vector.tensor_tensor(heads(probs[:, t, :]), heads(probs[:, t, :]),
                                        row_max[:, t, :].unsqueeze(2).to_broadcast([P, HEADS, S]),
                                        ALU.subtract).then_inc(s_less_max, 1)

            def mask_and_max(i, t):
                dve.wait_ge(s_mm, TILES * i + t + 1)
                for n in range(2):
                    last = nc.vector.scalar_tensor_tensor(
                        out=heads(probs[:, t, n * BANK:(n + 1) * BANK]), in0=heads(bank[(5 + 2 * t + n) % 8][:]),
                        scalar=beta[:, bass.ds(i * TILES + t, 1)],
                        in1=mask[:].unsqueeze(1).to_broadcast([P, HEADS // 2, S]), op0=ALU.mult, op1=ALU.add)
                last.then_inc(s_masked, 1)
                dve.wait_ge(s_masked, TILES * i + t + 1)
                nc.vector.tensor_reduce(row_max[:, t, :], heads(probs[:, t, :]), AX.X, ALU.max).then_inc(s_max, 1)

            def sums(i, t):
                dve.wait_ge(exp_done, TILES * i + t + 1)
                nc.vector.tensor_reduce(row_sum[:, t, :], heads(probs[:, t, :]), AX.X, ALU.add).then_inc(sum_done, 1)
                dve.wait_ge(sum_done, TILES * i + t + 1)
                nc.vector.reciprocal(row_inv[:, t, :], row_sum[:, t, :]).then_inc(inv_done, 1)
                if t == 1:
                    dve.wait_ge(inv_done, TILES * i + t + 1)
                    dve.wait_ge(probs_done, TILES * i + t)
                    nc.vector.tensor_tensor(heads(probs[:, t, :]), heads(probs[:, t, :]),
                                            row_inv[:, t, :].unsqueeze(2).to_broadcast([P, HEADS, S]),
                                            ALU.mult).then_inc(probs_done, 1)

            def step(i, more=True):
                dve.wait_ge(k_mm, i + 1)
                for h in range(2):
                    for b in range(SEQT):
                        last = place_k(copy, 1, h, b)
                last.then_inc(k_placed_dve, 1)
                if more:
                    x_lo(i + 1)
                dve.wait_ge(q_mm, i + 1)
                for b in range(SEQT):
                    last = place_q(copy, 1, b)
                last.then_inc(q_placed_dve, 1)
                mask_and_max(i, 0)
                mask_and_max(i, 1)
                less_max(i, 1)
                sums(i, 0)
                sums(i, 1)
                for t in range(TILES):
                    dve.wait_ge(pT_mm, TILES * i + t + 1)
                    copy(probsT[:, t, BANK:2 * BANK], bank[(6 + 2 * t) % 8][:]).then_inc(pT_copied_dve, 1)
                    if more and t == 0:
                        sum_xa(i + 1)
                        scale_xa(i + 1)
                if more:
                    xa_lo_part(i + 1)
                for t in range(TILES):
                    dve.wait_ge(attn_hi_done, TILES * i + t + 1)
                    rest(attnT_lo[:, :, tok(t)], bank[1 + t][:].rearrange("p (c n) -> p c n", n=P),
                         attnT_hi[:, :, tok(t)]).then_inc(attn_split, 1)
                if more:
                    add_x(i + 1)
                x2_lo_part(i, 0)
                if more:
                    x1_parts(i + 1)
                x2_lo_part(i, 1)

            dve.wait_ge(small_loaded, 16 * SMALL_DMAS)
            dve.wait_ge(consts_step, 9)
            nc.vector.tensor_copy(idx0_f[:], idx0_all[:]).then_inc(tables_step, 1)
            for b in range(SEQT):
                nc.vector.tensor_scalar(beta[half(b), :], cond_all[half(b), b::SEQT], BETA_MAX,
                                        1.0 / math.sqrt(HD), ALU.min, ALU.mult).then_inc(tables_step, 1)
            dve.wait_ge(tables_step, 1 + SEQT)
            for n in range(ADAPTERS):
                nc.vector.tensor_scalar(scal_of[:, n, :], idx0_f[:], float(n), scal_all[:, n:n + 1],
                                        ALU.is_equal, ALU.mult).then_inc(tables_step, 1)
            dve.wait_ge(tables_step, 1 + SEQT + ADAPTERS)
            nc.vector.tensor_reduce(scal_sum[:], scal_of[:].rearrange("p n q -> p q n"), AX.X, ALU.add)\
                .then_inc(tables_step, 1)
            dve.wait_ge(tables_step, 2 + SEQT + ADAPTERS)
            rows = PSEQ * RANK
            nc.vector.tensor_tensor(scal_rows[:], scal_sum[0:rows, :].rearrange("p (i b) -> p i b", b=PSEQ),
                                    own_rows[:].unsqueeze(1).to_broadcast([rows, PAIRS, PSEQ]), ALU.mult)\
                .then_inc(tables_done, 1)
            dve.wait_ge(tables_done, 1)
            def take_matrix(k):
                for c, g in enumerate(groups_of(k)):
                    take_lo(g, w_lo[:, LOADED[k], c, :], w_hi[:, LOADED[k], c, :])

            x_lo(0)
            for c in range(NC):
                take_lo(c, w_lo[:, W0, c, :], w_hi[:, W0, c, :])
            take_lo(NC, a_all[:, :, 1, :], a_all[:, :, 0, :], "p (c n) -> p c n")
            take_lo(NC + 1, b_lo[:], b_hi[:])
            take_matrix(1)
            sum_xa(0)
            scale_xa(0)
            xa_lo_part(0)
            take_matrix(2)
            add_x(0)
            x1_parts(0)
            take_matrix(3)
            take_matrix(4)
            dve.wait_ge(zeroed, 3)
            with dve.Fori(0, PAIRS - 1) as i:
                step(i)
            step(PAIRS - 1, more=False)

        @block.gpsimd
        def _(pool):
            def add_identity(dst, src):
                return nc.gpsimd.tensor_tensor(dst[:], src[:], ident[:].unsqueeze(1).to_broadcast([P, TILES, P]),
                                               ALU.add)

            def build_w1(i):
                if not (isinstance(i, int) and i == 0):
                    pool.wait_ge(x1_mm, TILES * i)
                pool.wait_ge(w1_loaded, 16 * (1 + PSEQ) + 16 * PSEQ * i)
                add_identity(w1_bd, w1_in).then_inc(w1_ready, 1)

            def build_w3(i):
                pool.wait_ge(y_mm, 1 + TILES * i)
                pool.wait_ge(w3_loaded, 16 * (1 + PSEQ) + 16 * PSEQ * i)
                add_identity(w3_bd, w3_in).then_inc(w3_added, 1)

            def w3_lo_part(i):
                pool.wait_ge(w3_hi_done, i + 1)
                nc.gpsimd.tensor_tensor(w3_lo[:], w3_bd[:], w3_hi[:].bitcast(F32), ALU.subtract).then_inc(w3_ready, 1)

            def with_rows(op, t, rows, done):
                nc.gpsimd.tensor_tensor(heads(probs[:, t, :]), heads(probs[:, t, :]),
                                        rows[:, t, :].unsqueeze(2).to_broadcast([P, HEADS, S]), op).then_inc(done, 1)

            def step(i, more=True):
                build_w3(i)
                if more:
                    build_w1(i + 1)
                pool.wait_ge(s_max, TILES * i + 1)
                with_rows(ALU.subtract, 0, row_max, s_less_max)
                pool.wait_ge(inv_done, TILES * i + 1)
                with_rows(ALU.mult, 0, row_inv, probs_done)
                w3_lo_part(i)

            nc.gpsimd.memset(ident[:], 0.0).then_inc(consts_step, 1)
            nc.gpsimd.memset(block_mask[:], 0.0).then_inc(consts_step, 1)
            nc.gpsimd.memset(own_rows[:], 1.0).then_inc(consts_step, 1)
            pool.wait_ge(consts_step, 3)
            nc.gpsimd.affine_select(out=ident[:], in_=ident[:], compare_op=ALU.not_equal, fill=1.0, base=0,
                                    pattern=[[-1, P]], channel_multiplier=1).then_inc(consts_step, 1)
            nc.gpsimd.affine_select(out=block_mask[:], in_=block_mask[:], compare_op=ALU.is_ge, fill=MASKED, base=0,
                                    pattern=[[-1, P]], channel_multiplier=1).then_inc(consts_step, 1)
            nc.gpsimd.affine_select(out=own_rows[:], in_=own_rows[:], compare_op=ALU.is_ge, fill=0.0, base=0,
                                    pattern=[[-RANK, PSEQ]], channel_multiplier=1).then_inc(consts_step, 1)
            pool.wait_ge(consts_step, 6)
            nc.gpsimd.affine_select(out=own_rows[:], in_=own_rows[:], compare_op=ALU.is_ge, fill=0.0, base=RANK - 1,
                                    pattern=[[RANK, PSEQ]], channel_multiplier=-1).then_inc(consts_step, 1)
            pool.wait_ge(consts_step, 7)
            for b in range(SEQT):
                nc.gpsimd.tensor_copy(mask[half(b), :], block_mask[half(b), half(b)]).then_inc(consts_step, 1)
                pool.wait_ge(consts_step, 8 + b)
            nc.gpsimd.memset(w1_in[:], 0.0).then_inc(w_in_zeroed, 1)
            nc.gpsimd.memset(w3_in[:], 0.0).then_inc(w_in_zeroed, 1)
            for blocks in (k_bd, q_bd, v_bd):
                nc.gpsimd.memset(blocks[:], 0.0).then_inc(zeroed, 1)
            build_w1(0)
            with pool.Fori(0, PAIRS - 1) as i:
                step(i)
            step(PAIRS - 1, more=False)


_INS = ['x', 'itok_B_0_6', 'itok_B_1_198', 'cond_1', 'itok_B_0_7', 'L0_cond_W', 'L0_cond_A', 'L0_cond_Bm',
        'L0_cond_scalings', 'L1_cond_weights', 'L2_cond_Wq', 'L2_cond_Wk', 'L2_cond_Wv', 'L2_cond_Wo',
        'L3_cond_weights']
_OUTS = [((64, 64, 512), 'float32')]


def kernel(**inputs):
    import numpy as _np
    import concourse.bacc as _bacc
    from concourse import mybir as _mybir
    from concourse.bass_utils import run_bass_kernel_spmd as _run

    nc = _bacc.Bacc("TRN2", target_bir_lowering=False, num_devices=1)
    arrays, args = {}, []
    for name in _INS:
        a = _np.ascontiguousarray(inputs[name])
        arrays[f"in_{name}_dram"] = a
        args.append(nc.dram_tensor(f"in_{name}_dram", a.shape, _mybir.dt.from_np(a.dtype), kind="ExternalInput").ap())
    for i, (shape, dtype) in enumerate(_OUTS):
        dt = _mybir.dt.from_np(_np.dtype(dtype))
        args.append(nc.dram_tensor(f"out_{i}_dram", shape, dt, kind="ExternalOutput").ap())
    cond_resid_kernel(nc, *args)
    r = _run(nc, [arrays], core_ids=[0])
    got = tuple(r.results[0][f"out_{i}_dram"] for i in range(len(_OUTS)))
    return got[0]
```

```python
import math
from contextlib import ExitStack

import concourse.bass as bass
from concourse import mybir

F32 = mybir.dt.float32
F32R = mybir.dt.float32r
I32 = mybir.dt.int32
ALU = mybir.AluOpType
ACT = mybir.ActivationFunctionType
AX = mybir.AxisListType

P = 128
SEQS, S, D = 64, 64, 512
NC = D // P
TILES = 2
PT = TILES * P
PAIRS = SEQS * S // PT
PSEQ = PT // S
SEQT = P // S
HEADS, HD = 16, 32
HP = HEADS // 2
ADAPTERS, RANK = 8, 16
MASKED = -1.0e30
BETA_MAX = 4.0
BANK = 512
NW = 5
W0, WQ, WK, WV, WO = range(NW)
LOADED = (W0, WK, WQ, WV, WO)
STAGES = 3


def cond_resid_kernel(nc, x, idx0, idx1, cond, idx3, W, A, Bm, scal, w1, Wq, Wk, Wv, Wo, w3, out):
    weights = {W0: W, WQ: Wq, WK: Wk, WV: Wv, WO: Wo}
    x_v = x.rearrange("(i t b) s d -> i (b s) t d", t=TILES, b=SEQT)
    out_v = out.rearrange("(i t b) s d -> i (b s) t d", t=TILES, b=SEQT)

    b_parts = nc.dram_tensor("b_parts", [2, ADAPTERS * RANK, D], F32, kind="Internal").ap()

    with ExitStack() as ctx:
        def sb(name, shape, dt=F32):
            return ctx.enter_context(nc.sbuf_tensor(name, shape, dt))

        def sem(name):
            return ctx.enter_context(nc.semaphore(name))

        ctx.enter_context(nc.allow_non_contiguous_dma(reason="a few small tables are loaded once"))

        ident = sb("ident", [P, P])
        mask = sb("mask", [P, S])
        block_mask = sb("block_mask", [P, P])
        idx0_row = sb("idx0_row", [1, SEQS], I32)
        idx0_all = sb("idx0_all", [P, SEQS], I32)
        idx0_f = sb("idx0_f", [P, SEQS])
        scal_all = sb("scal_all", [P, ADAPTERS])
        scal_sum = sb("scal_sum", [P, SEQS])
        own_rows = sb("own_rows", [PSEQ * RANK, PSEQ])
        scal_rows = sb("scal_rows", [PSEQ * RANK, PAIRS, PSEQ])
        idx1_row = sb("idx1_row", [1, SEQS], I32)
        idx3_row = sb("idx3_row", [1, SEQS], I32)
        cond_all = sb("cond_all", [P, SEQS])
        beta = sb("beta", [P, PAIRS * TILES])
        w_hi = sb("w_hi", [P, NW, NC, D], F32R)
        w_lo = sb("w_lo", [P, NW, NC, D], F32R)
        a_all = sb("a_all", [P, NC, 2, P], F32R)
        b_hi = sb("b_hi", [P, D], F32R)
        b_lo = sb("b_lo", [P, D], F32R)

        x_in = sb("x_in", [P, TILES, D])
        xT_hi = sb("xT_hi", [P, NC, PT], F32R)
        xT_lo = sb("xT_lo", [P, NC, PT], F32R)
        a_sel = sb("a_sel", [P, NC, 2, PSEQ * RANK], F32R)
        b_sel = sb("b_sel", [3 * SEQT * RANK, TILES, D], F32R)
        xa_low = sb("xa_low", [PSEQ * RANK, PT])
        xa_sum = sb("xa_sum", [PSEQ * RANK, PT])
        xa = sb("xa", [PSEQ * RANK, PT])
        xa_hi = sb("xa_hi", [PSEQ * RANK, PT], F32R)
        xa_parts = sb("xa_parts", [3 * SEQT * RANK, TILES, P], F32R)
        x0_hi = sb("x0_hi", [P, TILES, D], F32R)
        x0_lo = sb("x0_lo", [P, TILES, D], F32R)
        x1_both = sb("x1_both", [P, 2, TILES, D])
        x1 = x1_both[:, 0]
        x1_kept = x1_both[:, 1]
        x1T_hi = sb("x1T_hi", [P, NC, PT], F32R)
        x1T_lo = sb("x1T_lo", [P, NC, PT], F32R)
        q_bd = sb("q_bd", [P, TILES, HP, P])
        k_bd = sb("k_bd", [P, TILES, HP, P])
        v_bd = sb("v_bd", [P, TILES, SEQT, HP, 2 * HD])
        probs = sb("probs", [P, TILES, HEADS * S])
        row_max = sb("row_max", [P, TILES, HEADS])
        row_sum = sb("row_sum", [P, TILES, HEADS])
        row_inv = sb("row_inv", [P, TILES, HEADS])
        probsT = sb("probsT", [P, TILES, HP * P])
        attnT_hi = sb("attnT_hi", [P, NC, PT], F32R)
        attnT_lo = sb("attnT_lo", [P, NC, PT], F32R)
        x2_hi = sb("x2_hi", [P, TILES, D], F32R)
        x2_lo = sb("x2_lo", [P, TILES, D], F32R)
        x2 = probs[:, :, 0:D]
        y = sb("y", [P, TILES, D])
        x0 = y
        w1_in = sb("w1_in", [P, TILES, P])
        w3_in = sb("w3_in", [P, TILES, P])
        w1_bd = sb("w1_bd", [P, TILES, P])
        w1_hi = sb("w1_hi", [P, TILES, P], F32R)
        w1_lo = sb("w1_lo", [P, TILES, P], F32R)
        w3_bd = sb("w3_bd", [P, TILES, P])
        w3_hi = sb("w3_hi", [P, TILES, P], F32R)
        w3_lo = sb("w3_lo", [P, TILES, P], F32R)
        scal_of = y[:, 0, :].rearrange("p (n q) -> p n q", q=SEQS)
        a_nat = y[:, 0, :]
        b_nat = y[:, 1, :].rearrange("p (c n) -> p c n", c=NC)
        stage = [probsT[:].rearrange("p t (c d) -> p (t c) d", d=D),
                 probs[:].rearrange("p t (c d) -> p (t c) d", d=D),
                 x1_both[:].rearrange("p a t d -> p (a t) d")]

        banks = ctx.enter_context(nc.psum_tensor("banks", [P, 8 * BANK], F32))
        bank = [banks[:, b * BANK:(b + 1) * BANK] for b in range(8)]
        banks_23 = banks[:, 2 * BANK:4 * BANK]
        banks_56 = banks[:, 5 * BANK:7 * BANK]

        small_loaded = sem("small_loaded")
        ab_loaded = sem("ab_loaded")
        w_loaded = [sem(f"w_loaded{k}") for k in range(NW)]
        x_loaded = sem("x_loaded")
        b_parts_stored = sem("b_parts_stored")
        b_loaded = sem("b_loaded")
        w1_loaded = sem("w1_loaded")
        w3_loaded = sem("w3_loaded")
        y_stored = sem("y_stored")
        consts_step = sem("consts_step")
        w_in_zeroed = sem("w_in_zeroed")
        zeroed = sem("zeroed")
        turned = sem("turned")
        turned_hi = sem("turned_hi")
        turned_lo = sem("turned_lo")
        tables_step = sem("tables_step")
        tables_done = sem("tables_done")
        xT_mm = sem("xT_mm")
        xa_mm = sem("xa_mm")
        x0_mm = sem("x0_mm")
        x1_mm = sem("x1_mm")
        x1T_mm = sem("x1T_mm")
        k_mm = sem("k_mm")
        q_mm = sem("q_mm")
        v_mm = sem("v_mm")
        s_mm = sem("s_mm")
        pT_mm = sem("pT_mm")
        av_mm = sem("av_mm")
        x2_mm = sem("x2_mm")
        y_mm = sem("y_mm")
        xT_hi_done = sem("xT_hi_done")
        xT_split = sem("xT_split")
        a_ready = sem("a_ready")
        xa_low_done = sem("xa_low_done")
        xa_summed = sem("xa_summed")
        xa_scaled = sem("xa_scaled")
        xa_hi_done = sem("xa_hi_done")
        xa_hi_placed = sem("xa_hi_placed")
        xa_lo_placed = sem("xa_lo_placed")
        x0_done = sem("x0_done")
        x0_hi_done = sem("x0_hi_done")
        x0_split = sem("x0_split")
        x1_copied = sem("x1_copied")
        x1_kept_done = sem("x1_kept_done")
        x1_hi_done = sem("x1_hi_done")
        x1_split = sem("x1_split")
        k_placed_act = sem("k_placed_act")
        k_placed_dve = sem("k_placed_dve")
        q_placed_act = sem("q_placed_act")
        q_placed_dve = sem("q_placed_dve")
        v_placed = sem("v_placed")
        s_masked = sem("s_masked")
        s_max = sem("s_max")
        s_less_max = sem("s_less_max")
        exp_done = sem("exp_done")
        sum_done = sem("sum_done")
        inv_done = sem("inv_done")
        probs_done = [sem(f"probs_done{t}") for t in range(TILES)]
        pT_copied_act = sem("pT_copied_act")
        pT_copied_dve = sem("pT_copied_dve")
        attn_hi_done = sem("attn_hi_done")
        attn_split = sem("attn_split")
        x2_added = sem("x2_added")
        x2_hi_done = sem("x2_hi_done")
        x2_split = sem("x2_split")
        y_copied = sem("y_copied")
        w1_added = sem("w1_added")
        w1_ready = sem("w1_ready")
        w3_added = sem("w3_added")
        w3_hi_done = sem("w3_hi_done")
        w3_ready = sem("w3_ready")

        SMALL_DMAS = 4
        AB_DMAS = 1 + NC
        GROUPS_BEFORE_PAIR0 = NC + 2
        GROUPS = NW * NC + 2

        ring = [3, 4, 5, 6, 7, 5]
        ring += [5 + (g + 1) % 3 for g in range((NW - 2) * NC)]
        ring += [1 + g for g in range(NC)]

        def bank_of_group(g):
            return bank[ring[g]]

        def groups_of(k):
            first = GROUPS_BEFORE_PAIR0 + (k - 1) * NC
            return range(first, first + NC)

        def heads(ap):
            return ap.rearrange("p (h k) -> p h k", k=S)

        def tok(t):
            return slice(t * P, (t + 1) * P)

        def half(b):
            return slice(b * 64, (b + 1) * 64)

        def place_k(copy, r, h, b):
            row = r * 64 + h * HD
            src = banks_56[row:row + HD, :].rearrange("p (m t b s) -> p b t m s", m=NC, t=TILES, b=SEQT)[:, b]
            return copy(k_bd[b * 64 + h * HD:b * 64 + (h + 1) * HD, :, r::2, h * S:(h + 1) * S], src)

        def place_q(copy, r, b):
            src = banks_23[half(r), :].rearrange("p (m t b s) -> p b t m s", m=NC, t=TILES, b=SEQT)[:, b]
            return copy(q_bd[half(b), :, r::2, b * S:(b + 1) * S], src)

        def place_v(copy, t, b, h):
            src = bank[4 if t == 0 else 1][half(b), :].rearrange("p (m h e) -> p h m e", h=2, e=HD)[:, h]
            return copy(v_bd[half(h), t, b, :, h * HD:(h + 1) * HD], src)

        block = ctx.enter_context(nc.Block())

        @block.sync
        def _(sp):
            for counted_from_one in (y_copied, y_stored, w3_added, y_mm):
                sp.sem_inc(counted_from_one, 1)
            sp.dma_start(x_in[:], x_v[0]).then_inc(x_loaded, 16)
            sp.dma_start(stage[0], W.rearrange("(c p) d -> p c d", p=P)).then_inc(w_loaded[0], 16)
            sp.dma_start(a_nat, A.rearrange("n r d -> (n r) d")).then_inc(ab_loaded, 16)
            for c in range(NC):
                sp.dma_start(b_nat[:, c, :].rearrange("p (n r) -> p n r", r=RANK),
                             Bm[:, c * P:(c + 1) * P, :].rearrange("n p r -> p n r")).then_inc(ab_loaded, 16)
            sp.dma_start(idx1_row[:], idx1.rearrange("(a n) -> a n", a=1)).then_inc(w1_loaded, 16)
            sp.dma_start(idx3_row[:], idx3.rearrange("(a n) -> a n", a=1)).then_inc(w3_loaded, 16)
            sp.dma_start(idx0_row[:], idx0.rearrange("(a n) -> a n", a=1)).then_inc(small_loaded, 16)
            sp.dma_start(idx0_all[:], idx0.partition_broadcast(P)).then_inc(small_loaded, 16)
            sp.dma_start(cond_all[:], cond.rearrange("n a -> (n a)").partition_broadcast(P)).then_inc(small_loaded, 16)
            sp.dma_start(scal_all[:], scal.partition_broadcast(P)).then_inc(small_loaded, 16)
            for k in (1, 2):
                sp.dma_start(stage[k], weights[LOADED[k]].rearrange("(c p) d -> p c d", p=P))\
                    .then_inc(w_loaded[k], 16)

            def pair_indices(row, rows, i):
                return [sp.value_load(row[0:1, bass.ds(i * PSEQ + n, 1)], min_val=0, max_val=rows - 1)
                        for n in range(PSEQ)]

            def gather(dst, table, at, arrived):
                for n in range(PSEQ):
                    t, b = divmod(n, SEQT)
                    sp.dma_start(dst[half(b), t, half(b)], table[bass.ds(at[n], 1), :, :].rearrange("a c e -> (a c) e"))\
                        .then_inc(arrived, 16)

            def gather_b(at):
                for n in range(PSEQ):
                    t, b = divmod(n, SEQT)
                    for k, part in enumerate((0, 0, 1)):
                        row = (k * SEQT + b) * RANK
                        sp.dma_start(b_sel[row:row + RANK, t, :].bitcast(F32),
                                     b_parts[part, bass.ds(at[n] * RANK, RANK), :]).then_inc(b_loaded, 16)

            def load_matrix(k):
                sp.wait_ge(turned, NC if k == STAGES else groups_of(k - STAGES)[-1] + 1)
                sp.dma_start(stage[k % STAGES], weights[LOADED[k]].rearrange("(c p) d -> p c d", p=P))\
                    .then_inc(w_loaded[k], 16)

            load_matrix(3)
            sp.wait_ge(w_in_zeroed, 2)
            sp.wait_ge(w1_loaded, 16)
            conditions_of_pair0 = pair_indices(idx1_row, w1.shape[0], 0)
            sp.wait_ge(turned_lo, GROUPS_BEFORE_PAIR0)
            for part, b_part in enumerate((b_hi, b_lo)):
                sp.dma_start(b_parts[part], b_part[:].bitcast(F32)).then_inc(b_parts_stored, 16)
            gather(w1_in, w1, conditions_of_pair0, w1_loaded)
            sp.wait_ge(small_loaded, 16 * SMALL_DMAS)
            adapters_of_pair0 = pair_indices(idx0_row, ADAPTERS, 0)
            sp.wait_ge(b_parts_stored, 16 * 2)
            gather_b(adapters_of_pair0)
            load_matrix(4)
            sp.wait_ge(w3_loaded, 16)
            gather(w3_in, w3, pair_indices(idx3_row, w3.shape[0], 0), w3_loaded)
            sp.wait_ge(x0_done, TILES)
            sp.dma_start(x_in[:], x_v[1]).then_inc(x_loaded, 16)
            gather_b(pair_indices(idx0_row, ADAPTERS, 1))

            def step(i, left):
                if left >= 1:
                    at1 = pair_indices(idx1_row, w1.shape[0], i + 1)
                    at3 = pair_indices(idx3_row, w3.shape[0], i + 1)
                    sp.wait_ge(w1_ready, i + 1)
                    gather(w1_in, w1, at1, w1_loaded)
                    sp.wait_ge(w3_added, 1 + (i + 1))
                    gather(w3_in, w3, at3, w3_loaded)
                if left >= 2:
                    at0 = pair_indices(idx0_row, ADAPTERS, i + 2)
                    sp.wait_ge(x0_done, TILES * (i + 2))
                    sp.dma_start(x_in[:], x_v[i + 2] if isinstance(i, int)
                                 else x_v[bass.ds(i + 2, 1)].rearrange("a p t d -> (a p) t d")).then_inc(x_loaded, 16)
                    gather_b(at0)
                sp.wait_ge(y_copied, 1 + TILES * (i + 1))
                sp.dma_start(out_v[i] if isinstance(i, int)
                             else out_v[bass.ds(i, 1)].rearrange("a p t d -> (a p) t d"), y[:]).then_inc(y_stored, 16)

            with sp.Fori(0, PAIRS - 2) as i:
                step(i, 2)
            step(PAIRS - 2, 1)
            step(PAIRS - 1, 0)
            sp.wait_ge(y_stored, 1 + 16 * PAIRS)

        @block.tensor
        def _(pe):
            def turn(g, pieces):
                before = [n for n in range(g) if ring[n] == ring[g]]
                if before:
                    pe.wait_ge(turned_lo, before[-1] + 1)
                for c, piece in enumerate(pieces):
                    last = nc.tensor.transpose(bank_of_group(g)[:, c * P:(c + 1) * P], piece, ident[:])
                last.then_inc(turned, 1)

            def turn_matrix(k, g):
                pe.wait_ge(w_loaded[k], 16)
                for dc in range(NC):
                    turn(g + dc, [stage[k % STAGES][:, oc, dc * P:(dc + 1) * P] for oc in range(NC)])

            def split_products(out_ap, pairs):
                n = len(pairs)
                for k, (s_hi, s_lo, m_hi, m_lo) in enumerate(pairs):
                    nc.tensor.matmul(out_ap, s_hi, m_hi, start=(k == 0), stop=False)
                    nc.tensor.matmul(out_ap, s_hi, m_lo, start=False, stop=False)
                    last = nc.tensor.matmul(out_ap, s_lo, m_hi, start=False, stop=(k == n - 1))
                return last

            def turn_x(i):
                pe.wait_ge(x_loaded, 16 * (i + 1))
                if not (isinstance(i, int) and i == 0):
                    pe.wait_ge(y_copied, 1 + TILES * (i - 1))
                for t in range(TILES):
                    for c in range(NC):
                        last = nc.tensor.transpose(bank[t][:, c * P:(c + 1) * P],
                                                   x_in[:, t, c * P:(c + 1) * P], ident[:])
                    last.then_inc(xT_mm, 1)

            def adapters_down(i):
                pe.wait_ge(a_ready, i + 1)
                pe.wait_ge(xT_split, TILES * (i + 1))
                for c in range(NC):
                    for part in (xT_hi, xT_lo):
                        last = nc.tensor.matmul(bank[2][:, 0:PT], a_sel[:, c, :, :].rearrange("p a n -> p (a n)"),
                                                part[:, c, :], start=(c == 0 and part is xT_hi),
                                                stop=(c == NC - 1 and part is xT_lo))
                last.then_inc(xa_mm, 1)

            def layer0_dense(t, chunks=range(NC)):
                for c in chunks:
                    nc.tensor.matmul(bank[3 + t][:], xT_hi[:, c, tok(t)], w_hi[:, W0, c, :],
                                     start=(c == 0), stop=False)
                    nc.tensor.matmul(bank[3 + t][:], xT_hi[:, c, tok(t)], w_lo[:, W0, c, :],
                                     start=False, stop=False)
                    nc.tensor.matmul(bank[3 + t][:], xT_lo[:, c, tok(t)], w_hi[:, W0, c, :],
                                     start=False, stop=False)

            def adapters_up(i):
                pe.wait_ge(b_loaded, 16 * 3 * PSEQ * (i + 1))
                pe.wait_ge(xa_hi_placed, i + 1)
                pe.wait_ge(xa_lo_placed, i + 1)
                for t in range(TILES):
                    nc.tensor.matmul(bank[3 + t][:], xa_parts[:, t, :], b_sel[:, t, :],
                                     start=False, stop=True).then_inc(x0_mm, 1)

            def layer1(i):
                pe.wait_ge(w1_ready, i + 1)
                for t in range(TILES):
                    pe.wait_ge(x0_hi_done, TILES * i + t + 1)
                    nc.tensor.matmul(bank[3 + t][:], w1_hi[:, t, :], x0_hi[:, t, :], start=True, stop=False)
                    nc.tensor.matmul(bank[3 + t][:], w1_lo[:, t, :], x0_hi[:, t, :], start=False, stop=False)
                    pe.wait_ge(x0_split, TILES * i + t + 1)
                    nc.tensor.matmul(bank[3 + t][:], w1_hi[:, t, :], x0_lo[:, t, :], start=False, stop=True)\
                        .then_inc(x1_mm, 1)

            def turn_x1(i):
                for t in range(TILES):
                    pe.wait_ge(x1_copied, TILES * i + t + 1)
                    for c in range(NC):
                        last = nc.tensor.transpose(bank[(7 + t) % 8][:, c * P:(c + 1) * P],
                                                   x1[:, t, c * P:(c + 1) * P], ident[:])
                    last.then_inc(x1T_mm, 1)

            def project_T(w, first_bank, m):
                return split_products(
                    bank[first_bank + m // 2][:, (m % 2) * PT:(m % 2 + 1) * PT],
                    [(w_hi[:, w, c, m * P:(m + 1) * P], w_lo[:, w, c, m * P:(m + 1) * P],
                      x1T_hi[:, c, :], x1T_lo[:, c, :]) for c in range(NC)])

            def keys(i, chunks):
                if chunks[0] == 0:
                    pe.wait_ge(x1_split, TILES * (i + 1))
                for m in chunks:
                    last = project_T(WK, 5, m)
                if chunks[-1] == NC - 1:
                    last.then_inc(k_mm, 1)

            def queries(i):
                pe.wait_ge(y_copied, 1 + TILES * i)
                for m in range(NC):
                    last = project_T(WQ, 2, m)
                last.then_inc(q_mm, 1)

            def values(t):
                split_products(bank[4 if t == 0 else 1][:],
                               [(x1T_hi[:, c, tok(t)], x1T_lo[:, c, tok(t)], w_hi[:, WV, c, :], w_lo[:, WV, c, :])
                                for c in range(NC)]).then_inc(v_mm, 1)

            def scores(i, t):
                if t == 0:
                    for placed in (k_placed_act, k_placed_dve, q_placed_act, q_placed_dve):
                        pe.wait_ge(placed, i + 1)
                for hp in range(HP):
                    b = (5 + 2 * t + hp // 4) % 8
                    last = nc.tensor.matmul(bank[b][:, hp % 4 * P:(hp % 4 + 1) * P], q_bd[:, t, hp, :],
                                            k_bd[:, t, hp, :], start=True, stop=True)
                    if hp % 4 == 3:
                        last.then_inc(s_mm, 1)

            def turn_probs(i, t):
                pe.wait_ge(probs_done[t], i + 1)
                for hp in range(HP):
                    b = (5 + 2 * t + hp // 4) % 8
                    last = nc.tensor.transpose(bank[b][:, hp % 4 * P:(hp % 4 + 1) * P],
                                               probs[:, t, hp * P:(hp + 1) * P], ident[:])
                last.then_inc(pT_mm, 1)

            def attend(i, t):
                pe.wait_ge(pT_copied_act, TILES * i + t + 1)
                pe.wait_ge(pT_copied_dve, TILES * i + t + 1)
                if t == 0:
                    pe.wait_ge(v_placed, TILES * (i + 1))
                for hp in range(HP):
                    for b in range(SEQT):
                        at = hp * P + b * S
                        last = nc.tensor.matmul(
                            bank[1 + t][half(hp % 2), hp // 2 * P + b * S:hp // 2 * P + (b + 1) * S],
                            v_bd[:, t, b, hp, :], probsT[:, t, at:at + S], start=True, stop=True)
                last.then_inc(av_mm, 1)

            def layer2_out_hi(i, t, chunks=range(NC)):
                if chunks[0] == 0:
                    pe.wait_ge(attn_hi_done, TILES * i + t + 1)
                for c in chunks:
                    for m in (w_hi, w_lo):
                        nc.tensor.matmul(bank[5 + t][:], attnT_hi[:, c, tok(t)], m[:, WO, c, :],
                                         start=(c == 0 and m is w_hi), stop=False)

            def layer2_out_lo(i, t):
                pe.wait_ge(attn_split, TILES * i + t + 1)
                for c in range(NC):
                    last = nc.tensor.matmul(bank[5 + t][:], attnT_lo[:, c, tok(t)], w_hi[:, WO, c, :],
                                            start=False, stop=(c == NC - 1))
                last.then_inc(x2_mm, 1)

            def layer3(i, t):
                if t == 0:
                    pe.wait_ge(w3_ready, i + 1)
                pe.wait_ge(x2_split, TILES * i + t + 1)
                split_products(bank[1 + t][:],
                               [(w3_hi[:, t, :], w3_lo[:, t, :], x2_hi[:, t, :], x2_lo[:, t, :])]).then_inc(y_mm, 1)

            def step(i, more=True):
                if more:
                    turn_x(i + 1)
                queries(i)
                if more:
                    values(0)
                scores(i, 0)
                if more:
                    pe.wait_ge(xT_split, TILES * (i + 2))
                scores(i, 1)
                if not more:
                    values(0)
                values(1)
                if more:
                    adapters_down(i + 1)
                    pe.wait_ge(v_placed, TILES * i + 1)
                    layer0_dense(0)
                    layer0_dense(1, range(NC - 1))
                turn_probs(i, 0)
                if more:
                    layer0_dense(1, [NC - 1])
                turn_probs(i, 1)
                attend(i, 0)
                if more:
                    pe.wait_ge(xa_summed, i + 2)
                attend(i, 1)
                if more:
                    adapters_up(i + 1)
                layer2_out_hi(i, 0)
                layer2_out_lo(i, 0)
                if more:
                    layer1(i + 1)
                layer2_out_hi(i, 1, range(NC // 2))
                if more:
                    turn_x1(i + 1)
                layer2_out_hi(i, 1, range(NC // 2, NC))
                layer2_out_lo(i, 1)
                layer3(i, 0)
                if more:
                    keys(i + 1, [0, 1])
                layer3(i, 1)
                if more:
                    keys(i + 1, [2, 3])

            pe.wait_ge(consts_step, 9)
            turn_x(0)
            turn_matrix(0, 0)
            pe.wait_ge(ab_loaded, 16 * AB_DMAS)
            turn(NC, [a_nat[:, c * P:(c + 1) * P] for c in range(NC)])
            turn(NC + 1, [b_nat[:, c, :] for c in range(NC)])
            pe.wait_ge(turned_lo, NC)
            pe.wait_ge(xT_split, TILES)
            layer0_dense(0)
            turn_matrix(1, groups_of(1)[0])
            adapters_down(0)
            turn_matrix(2, groups_of(2)[0])
            layer0_dense(1)
            turn_matrix(3, groups_of(3)[0])
            adapters_up(0)
            layer1(0)
            pe.wait_ge(turned_lo, groups_of(3)[-1] + 1)
            turn_x1(0)
            turn_matrix(4, groups_of(4)[0])
            keys(0, range(NC))
            pe.wait_ge(turned_lo, GROUPS)
            with pe.Fori(0, PAIRS - 1) as i:
                step(i)
            step(PAIRS - 1, more=False)

        @block.scalar
        def _(act):
            def copy(dst, src):
                return nc.scalar.activation(dst, src, ACT.Copy)

            def take_hi(g, dst, view="p n -> p n"):
                act.wait_ge(turned, g + 1)
                sizes = {"c": NC} if "(" in view else {}
                copy(dst, bank_of_group(g)[:].rearrange(view, **sizes)).then_inc(turned_hi, 1)

            def x_hi(i):
                for t in range(TILES):
                    act.wait_ge(xT_mm, TILES * i + t + 1)
                    copy(xT_hi[:, :, tok(t)], bank[t][:].rearrange("p (c n) -> p c n", n=P)).then_inc(xT_hi_done, 1)

            def select_a(i):
                for n in range(PSEQ):
                    at = act.value_load(idx0_row[0:1, bass.ds(i * PSEQ + n, 1)], min_val=0, max_val=ADAPTERS - 1)
                    last = copy(a_sel[:, :, :, n * RANK:(n + 1) * RANK], a_all[:, :, :, bass.ds(at * RANK, RANK)])
                last.then_inc(a_ready, 1)

            def xa_low_part(i):
                act.wait_ge(xa_mm, i + 1)
                copy(xa_low[:], bank[2][half(1), 0:PT]).then_inc(xa_low_done, 1)

            def xa_hi_part(i):
                act.wait_ge(xa_scaled, i + 1)
                copy(xa_hi[:], xa[:]).then_inc(xa_hi_done, 1)
                act.wait_ge(xa_hi_done, i + 1)
                n = SEQT * RANK
                for t in range(TILES):
                    for part in (0, 2):
                        last = copy(xa_parts[part * n:(part + 1) * n, t, :], xa_hi[t * n:(t + 1) * n, tok(t)])
                last.then_inc(xa_hi_placed, 1)

            def x0_hi_part(i):
                for t in range(TILES):
                    act.wait_ge(x0_done, TILES * i + t + 1)
                    copy(x0_hi[:, t, :], x0[:, t, :]).then_inc(x0_hi_done, 1)

            def x1_copy(i):
                for t in range(TILES):
                    act.wait_ge(x1_mm, TILES * i + t + 1)
                    copy(x1[:, t, :], bank[3 + t][:]).then_inc(x1_copied, 1)

            def x1T_hi_part(i):
                for t in range(TILES):
                    act.wait_ge(x1T_mm, TILES * i + t + 1)
                    copy(x1T_hi[:, :, tok(t)], bank[(7 + t) % 8][:].rearrange("p (c n) -> p c n", n=P))\
                        .then_inc(x1_hi_done, 1)

            def keep_x1(i):
                act.wait_ge(x1_copied, TILES * (i + 1))
                copy(x1_kept[:], x1[:]).then_inc(x1_kept_done, 1)

            def place_heads(i):
                act.wait_ge(k_mm, i + 1)
                for h in range(2):
                    for b in range(SEQT):
                        last = place_k(copy, 0, h, b)
                last.then_inc(k_placed_act, 1)

            def place_queries(i):
                act.wait_ge(q_mm, i + 1)
                for b in range(SEQT):
                    last = place_q(copy, 0, b)
                last.then_inc(q_placed_act, 1)

            def place_values(i, t):
                act.wait_ge(v_mm, TILES * i + t + 1)
                for b in range(SEQT):
                    for h in range(2):
                        last = place_v(copy, t, b, h)
                last.then_inc(v_placed, 1)

            def exp(i, t):
                act.wait_ge(s_less_max, TILES * i + t + 1)
                nc.scalar.activation(probs[:, t, :], probs[:, t, :], ACT.Exp).then_inc(exp_done, 1)

            def x2_hi_part(i, t):
                act.wait_ge(x2_added, TILES * i + t + 1)
                copy(x2_hi[:, t, :], x2[:, t, :]).then_inc(x2_hi_done, 1)

            def step(i, more=True):
                place_heads(i)
                if more:
                    x_hi(i + 1)
                    select_a(i + 1)
                keep_x1(i)
                place_queries(i)
                if more:
                    place_values(i, 0)
                act.wait_ge(w3_added, 1 + i + 1)
                copy(w3_hi[:], w3_bd[:]).then_inc(w3_hi_done, 1)
                exp(i, 0)
                if more:
                    xa_low_part(i + 1)
                    place_values(i, 1)
                exp(i, 1)
                if not more:
                    place_values(i, 0)
                    place_values(i, 1)
                for t in range(TILES):
                    act.wait_ge(pT_mm, TILES * i + t + 1)
                    copy(probsT[:, t, 0:BANK], bank[(5 + 2 * t) % 8][:]).then_inc(pT_copied_act, 1)
                if more:
                    xa_hi_part(i + 1)
                for t in range(TILES):
                    act.wait_ge(av_mm, TILES * i + t + 1)
                    copy(attnT_hi[:, :, tok(t)], bank[1 + t][:].rearrange("p (c n) -> p c n", n=P))\
                        .then_inc(attn_hi_done, 1)
                if more:
                    x0_hi_part(i + 1)
                    x1_copy(i + 1)
                x2_hi_part(i, 0)
                if more:
                    x1T_hi_part(i + 1)
                x2_hi_part(i, 1)
                act.wait_ge(y_stored, 1 + 16 * i)
                for t in range(TILES):
                    act.wait_ge(y_mm, 1 + TILES * i + t + 1)
                    copy(y[:, t, :], bank[1 + t][:]).then_inc(y_copied, 1)

            def take_matrix(k):
                for c, g in enumerate(groups_of(k)):
                    take_hi(g, w_hi[:, LOADED[k], c, :])

            x_hi(0)
            for c in range(NC):
                take_hi(c, w_hi[:, W0, c, :])
            take_hi(NC, a_all[:, :, 0, :], "p (c n) -> p c n")
            take_hi(NC + 1, b_hi[:])
            act.wait_ge(turned_lo, NC + 1)
            act.wait_ge(small_loaded, 16 * SMALL_DMAS)
            select_a(0)
            take_matrix(1)
            xa_low_part(0)
            take_matrix(2)
            xa_hi_part(0)
            take_matrix(3)
            x0_hi_part(0)
            x1_copy(0)
            x1T_hi_part(0)
            take_matrix(4)
            act.wait_ge(zeroed, 3)
            with act.Fori(0, PAIRS - 1) as i:
                step(i)
            step(PAIRS - 1, more=False)

        @block.vector
        def _(dve):
            def copy(dst, src):
                return nc.vector.tensor_copy(dst, src)

            def rest(dst, whole, hi):
                return nc.vector.tensor_tensor(dst, whole, hi.bitcast(F32), ALU.subtract)

            def take_lo(g, dst, hi, view="p n -> p n"):
                dve.wait_ge(turned_hi, g + 1)
                sizes = {"c": NC} if "(" in view else {}
                rest(dst, bank_of_group(g)[:].rearrange(view, **sizes), hi).then_inc(turned_lo, 1)

            def x_lo(i):
                for t in range(TILES):
                    dve.wait_ge(xT_hi_done, TILES * i + t + 1)
                    rest(xT_lo[:, :, tok(t)], bank[t][:].rearrange("p (c n) -> p c n", n=P),
                         xT_hi[:, :, tok(t)]).then_inc(xT_split, 1)

            def sum_xa(i):
                dve.wait_ge(xa_low_done, i + 1)
                nc.vector.tensor_tensor(xa_sum[:], bank[2][half(0), 0:PT], xa_low[:], ALU.add).then_inc(xa_summed, 1)

            def scale_xa(i):
                dve.wait_ge(xa_summed, i + 1)
                nc.vector.tensor_tensor(
                    xa[:].rearrange("p (b s) -> p b s", s=S), xa_sum[:].rearrange("p (b s) -> p b s", s=S),
                    scal_rows[:, bass.ds(i, 1), :].rearrange("p a b -> p (a b)").unsqueeze(2)
                    .to_broadcast([PSEQ * RANK, PSEQ, S]), ALU.mult).then_inc(xa_scaled, 1)

            def xa_lo_part(i):
                dve.wait_ge(xa_hi_done, i + 1)
                n = SEQT * RANK
                for t in range(TILES):
                    rows = slice(t * n, (t + 1) * n)
                    last = rest(xa_parts[n:2 * n, t, :], xa[rows, tok(t)], xa_hi[rows, tok(t)])
                last.then_inc(xa_lo_placed, 1)

            def add_x(i):
                if not (isinstance(i, int) and i == 0):
                    dve.wait_ge(y_stored, 1 + 16 * (i - 1))
                for t in range(TILES):
                    dve.wait_ge(x0_mm, TILES * i + t + 1)
                    nc.vector.tensor_tensor(x0[:, t, :], bank[3 + t][:], x_in[:, t, :], ALU.add)\
                        .then_inc(x0_done, 1)

            def x0_lo_part(i):
                for t in range(TILES):
                    dve.wait_ge(x0_hi_done, TILES * i + t + 1)
                    rest(x0_lo[:, t, :], x0[:, t, :], x0_hi[:, t, :]).then_inc(x0_split, 1)

            def x1T_lo_part(i):
                for t in range(TILES):
                    dve.wait_ge(x1_hi_done, TILES * i + t + 1)
                    rest(x1T_lo[:, :, tok(t)], bank[(7 + t) % 8][:].rearrange("p (c n) -> p c n", n=P),
                         x1T_hi[:, :, tok(t)]).then_inc(x1_split, 1)

            def add_x1(i, t):
                dve.wait_ge(x1_kept_done, i + 1)
                dve.wait_ge(x2_mm, TILES * i + t + 1)
                nc.vector.tensor_tensor(x2[:, t, :], bank[5 + t][:], x1_kept[:, t, :], ALU.add)\
                    .then_inc(x2_added, 1)

            def x2_lo_part(i, t):
                dve.wait_ge(x2_hi_done, TILES * i + t + 1)
                rest(x2_lo[:, t, :], x2[:, t, :], x2_hi[:, t, :]).then_inc(x2_split, 1)

            def mask_and_max(i, t):
                for n in range(2):
                    dve.wait_ge(s_mm, 2 * TILES * i + 2 * t + n + 1)
                    last = nc.vector.scalar_tensor_tensor(
                        out=heads(probs[:, t, n * BANK:(n + 1) * BANK]), in0=heads(bank[(5 + 2 * t + n) % 8][:]),
                        scalar=beta[:, bass.ds(i * TILES + t, 1)],
                        in1=mask[:].unsqueeze(1).to_broadcast([P, HEADS // 2, S]), op0=ALU.mult, op1=ALU.add)
                last.then_inc(s_masked, 1)
                dve.wait_ge(s_masked, TILES * i + t + 1)
                nc.vector.tensor_reduce(row_max[:, t, :], heads(probs[:, t, :]), AX.X, ALU.max).then_inc(s_max, 1)

            def sums(i, t):
                dve.wait_ge(exp_done, TILES * i + t + 1)
                nc.vector.tensor_reduce(row_sum[:, t, :], heads(probs[:, t, :]), AX.X, ALU.add).then_inc(sum_done, 1)
                dve.wait_ge(sum_done, TILES * i + t + 1)
                nc.vector.reciprocal(row_inv[:, t, :], row_sum[:, t, :]).then_inc(inv_done, 1)
                if t == 1:
                    dve.wait_ge(inv_done, TILES * i + t + 1)
                    nc.vector.tensor_tensor(heads(probs[:, t, :]), heads(probs[:, t, :]),
                                            row_inv[:, t, :].unsqueeze(2).to_broadcast([P, HEADS, S]),
                                            ALU.mult).then_inc(probs_done[t], 1)

            def step(i, more=True):
                dve.wait_ge(k_mm, i + 1)
                for h in range(2):
                    for b in range(SEQT):
                        last = place_k(copy, 1, h, b)
                last.then_inc(k_placed_dve, 1)
                if more:
                    x_lo(i + 1)
                dve.wait_ge(q_mm, i + 1)
                for b in range(SEQT):
                    last = place_q(copy, 1, b)
                last.then_inc(q_placed_dve, 1)
                mask_and_max(i, 0)
                mask_and_max(i, 1)
                sums(i, 0)
                sums(i, 1)
                for t in range(TILES):
                    dve.wait_ge(pT_mm, TILES * i + t + 1)
                    copy(probsT[:, t, BANK:2 * BANK], bank[(6 + 2 * t) % 8][:]).then_inc(pT_copied_dve, 1)
                    if more and t == 0:
                        sum_xa(i + 1)
                        scale_xa(i + 1)
                if more:
                    xa_lo_part(i + 1)
                for t in range(TILES):
                    dve.wait_ge(attn_hi_done, TILES * i + t + 1)
                    rest(attnT_lo[:, :, tok(t)], bank[1 + t][:].rearrange("p (c n) -> p c n", n=P),
                         attnT_hi[:, :, tok(t)]).then_inc(attn_split, 1)
                if more:
                    add_x(i + 1)
                    x0_lo_part(i + 1)
                add_x1(i, 0)
                x2_lo_part(i, 0)
                if more:
                    x1T_lo_part(i + 1)
                add_x1(i, 1)
                x2_lo_part(i, 1)

            def take_matrix(k):
                for c, g in enumerate(groups_of(k)):
                    take_lo(g, w_lo[:, LOADED[k], c, :], w_hi[:, LOADED[k], c, :])

            x_lo(0)
            for c in range(NC):
                take_lo(c, w_lo[:, W0, c, :], w_hi[:, W0, c, :])
            take_lo(NC, a_all[:, :, 1, :], a_all[:, :, 0, :], "p (c n) -> p c n")
            take_lo(NC + 1, b_lo[:], b_hi[:])

            dve.wait_ge(small_loaded, 16 * SMALL_DMAS)
            dve.wait_ge(consts_step, 9)
            nc.vector.tensor_copy(idx0_f[:], idx0_all[:]).then_inc(tables_step, 1)
            for b in range(SEQT):
                nc.vector.tensor_scalar(beta[half(b), :], cond_all[half(b), b::SEQT], BETA_MAX,
                                        1.0 / math.sqrt(HD), ALU.min, ALU.mult).then_inc(tables_step, 1)
            dve.wait_ge(tables_step, 1 + SEQT)
            for n in range(ADAPTERS):
                nc.vector.tensor_scalar(scal_of[:, n, :], idx0_f[:], float(n), scal_all[:, n:n + 1],
                                        ALU.is_equal, ALU.mult).then_inc(tables_step, 1)
            dve.wait_ge(tables_step, 1 + SEQT + ADAPTERS)
            nc.vector.tensor_reduce(scal_sum[:], scal_of.rearrange("p n q -> p q n"), AX.X, ALU.add)\
                .then_inc(tables_step, 1)
            dve.wait_ge(tables_step, 2 + SEQT + ADAPTERS)
            rows = PSEQ * RANK
            nc.vector.tensor_tensor(scal_rows[:], scal_sum[0:rows, :].rearrange("p (i b) -> p i b", b=PSEQ),
                                    own_rows[:].unsqueeze(1).to_broadcast([rows, PAIRS, PSEQ]), ALU.mult)\
                .then_inc(tables_done, 1)
            dve.wait_ge(tables_done, 1)

            take_matrix(1)
            sum_xa(0)
            scale_xa(0)
            take_matrix(2)
            xa_lo_part(0)
            take_matrix(3)
            add_x(0)
            x0_lo_part(0)
            x1T_lo_part(0)
            take_matrix(4)
            dve.wait_ge(zeroed, 3)
            with dve.Fori(0, PAIRS - 1) as i:
                step(i)
            step(PAIRS - 1, more=False)

        @block.gpsimd
        def _(pool):
            def add_identity(dst, src):
                return nc.gpsimd.tensor_tensor(dst[:], src[:], ident[:].unsqueeze(1).to_broadcast([P, TILES, P]),
                                               ALU.add)

            def build_w1(i):
                if not (isinstance(i, int) and i == 0):
                    pool.wait_ge(x1_mm, TILES * i)
                pool.wait_ge(w1_loaded, 16 * (1 + PSEQ) + 16 * PSEQ * i)
                add_identity(w1_bd, w1_in).then_inc(w1_added, 1)
                add_identity(w1_hi, w1_in).then_inc(w1_added, 1)
                pool.wait_ge(w1_added, 2 * (i + 1))
                nc.gpsimd.tensor_tensor(w1_lo[:], w1_bd[:], w1_hi[:].bitcast(F32), ALU.subtract).then_inc(w1_ready, 1)

            def build_w3(i):
                pool.wait_ge(y_mm, 1 + TILES * i)
                pool.wait_ge(w3_loaded, 16 * (1 + PSEQ) + 16 * PSEQ * i)
                add_identity(w3_bd, w3_in).then_inc(w3_added, 1)

            def w3_lo_part(i):
                pool.wait_ge(w3_hi_done, i + 1)
                nc.gpsimd.tensor_tensor(w3_lo[:], w3_bd[:], w3_hi[:].bitcast(F32), ALU.subtract).then_inc(w3_ready, 1)

            def with_rows(op, t, rows, done):
                nc.gpsimd.tensor_tensor(heads(probs[:, t, :]), heads(probs[:, t, :]),
                                        rows[:, t, :].unsqueeze(2).to_broadcast([P, HEADS, S]), op).then_inc(done, 1)

            def step(i, more=True):
                build_w3(i)
                if more:
                    build_w1(i + 1)
                for t in range(TILES):
                    pool.wait_ge(s_max, TILES * i + t + 1)
                    with_rows(ALU.subtract, t, row_max, s_less_max)
                pool.wait_ge(inv_done, TILES * i + 1)
                with_rows(ALU.mult, 0, row_inv, probs_done[0])
                w3_lo_part(i)

            nc.gpsimd.memset(ident[:], 0.0).then_inc(consts_step, 1)
            nc.gpsimd.memset(block_mask[:], 0.0).then_inc(consts_step, 1)
            nc.gpsimd.memset(own_rows[:], 1.0).then_inc(consts_step, 1)
            pool.wait_ge(consts_step, 3)
            nc.gpsimd.affine_select(out=ident[:], in_=ident[:], compare_op=ALU.not_equal, fill=1.0, base=0,
                                    pattern=[[-1, P]], channel_multiplier=1).then_inc(consts_step, 1)
            nc.gpsimd.affine_select(out=block_mask[:], in_=block_mask[:], compare_op=ALU.is_ge, fill=MASKED, base=0,
                                    pattern=[[-1, P]], channel_multiplier=1).then_inc(consts_step, 1)
            nc.gpsimd.affine_select(out=own_rows[:], in_=own_rows[:], compare_op=ALU.is_ge, fill=0.0, base=0,
                                    pattern=[[-RANK, PSEQ]], channel_multiplier=1).then_inc(consts_step, 1)
            pool.wait_ge(consts_step, 6)
            nc.gpsimd.affine_select(out=own_rows[:], in_=own_rows[:], compare_op=ALU.is_ge, fill=0.0, base=RANK - 1,
                                    pattern=[[RANK, PSEQ]], channel_multiplier=-1).then_inc(consts_step, 1)
            pool.wait_ge(consts_step, 7)
            for b in range(SEQT):
                nc.gpsimd.tensor_copy(mask[half(b), :], block_mask[half(b), half(b)]).then_inc(consts_step, 1)
                pool.wait_ge(consts_step, 8 + b)
            nc.gpsimd.memset(w1_in[:], 0.0).then_inc(w_in_zeroed, 1)
            nc.gpsimd.memset(w3_in[:], 0.0).then_inc(w_in_zeroed, 1)
            for blocks in (k_bd, q_bd, v_bd):
                nc.gpsimd.memset(blocks[:], 0.0).then_inc(zeroed, 1)
            build_w1(0)
            with pool.Fori(0, PAIRS - 1) as i:
                step(i)
            step(PAIRS - 1, more=False)


_INS = ['x', 'itok_B_0_6', 'itok_B_1_198', 'cond_1', 'itok_B_0_7', 'L0_cond_W', 'L0_cond_A', 'L0_cond_Bm',
        'L0_cond_scalings', 'L1_cond_weights', 'L2_cond_Wq', 'L2_cond_Wk', 'L2_cond_Wv', 'L2_cond_Wo',
        'L3_cond_weights']
_OUTS = [((64, 64, 512), 'float32')]


def kernel(**inputs):
    import numpy as _np
    import concourse.bacc as _bacc
    from concourse import mybir as _mybir
    from concourse.bass_utils import run_bass_kernel_spmd as _run

    nc = _bacc.Bacc("TRN2", target_bir_lowering=False, num_devices=1)
    arrays, args = {}, []
    for name in _INS:
        a = _np.ascontiguousarray(inputs[name])
        arrays[f"in_{name}_dram"] = a
        args.append(nc.dram_tensor(f"in_{name}_dram", a.shape, _mybir.dt.from_np(a.dtype), kind="ExternalInput").ap())
    for i, (shape, dtype) in enumerate(_OUTS):
        dt = _mybir.dt.from_np(_np.dtype(dtype))
        args.append(nc.dram_tensor(f"out_{i}_dram", shape, dt, kind="ExternalOutput").ap())
    cond_resid_kernel(nc, *args)
    r = _run(nc, [arrays], core_ids=[0])
    got = tuple(r.results[0][f"out_{i}_dram"] for i in range(len(_OUTS)))
    return got[0]
```
